# Optimizing a Trainium2 kernel written in Bass

```python
import numpy as np
import jax
import jax.numpy as jnp

def _softmax(x, axis=-1):
    return jax.nn.softmax(x, axis=axis)

def _gelu(x):
    return jax.nn.gelu(x, approximate=True)

def _silu(x):
    return jax.nn.silu(x)

def _sigmoid(x):
    return jax.nn.sigmoid(x)

def _layernorm(x, axis=-1, eps=1e-05):
    m = jnp.mean(x, axis=axis, keepdims=True)
    v = jnp.var(x, axis=axis, keepdims=True)
    return (x - m) / jnp.sqrt(v + eps)

def _scatter_add(tgt, idx, src, axis=0):
    return tgt.at[idx].add(src)

def _segment_sum(src, seg, n):
    return jax.ops.segment_sum(src, seg, n)
kernel_name = 'mk_adj_ffn_d2_adj_r2_323420'

def setup_inputs(seed: int=0):
    np.random.seed(seed)
    _w = jnp.asarray

    def _rec_inputs():
        import jax
        import jax.numpy as jnp
        _gk = jax.random.key(seed)
        x = -0.0005207 + 1.001 * jax.random.normal(jax.random.fold_in(_gk, 1), (32, 256, 128), jnp.float32)
        _w = (1.0 + jnp.arange(256, dtype=jnp.float32)) ** (-0.5)
        _w = _w / _w.mean()
        _pij = jnp.clip(0.015625 * _w[:, None] * _w[None, :], 0.0, 1.0)
        _a = jax.random.uniform(jax.random.fold_in(_gk, 2), (32, 256, 256)) < _pij
        _a = jnp.logical_or(_a, jnp.swapaxes(_a, -1, -2))
        _a = jnp.logical_or(_a, jnp.eye(256, dtype=bool))
        _af = _a.astype(jnp.float32)
        _af = _af * jax.random.uniform(jax.random.fold_in(_gk, 3), (32, 256, 256), jnp.float32, 0.05, 1)
        adj = _af
        return (x, adj)
    x, adj = _rec_inputs()

    def _L0_gnn_setup():
        import jax, jax.numpy as jnp
        import numpy as np
        H = 4
        LN_EPS = 1e-05

        def _heads(x, B, N):
            return x.reshape(B, N, H, -1).transpose(0, 2, 1, 3)
        key = jax.random.key(seed)
        ks = jax.random.split(key, 6)
        B, N, IN, OUT = (4, 1024, 128, 128)
        return {'node_feats': jax.random.normal(ks[0], (B, N, IN), dtype=jnp.float32), 'adj_matrix': jax.random.uniform(ks[1], (B, N, N), dtype=jnp.float32), 'W_lin': jax.random.normal(ks[2], (IN, OUT), dtype=jnp.float32) * IN ** (-0.5), 'b_lin': jnp.zeros((OUT,), dtype=jnp.float32), 'W_q': jax.random.normal(ks[3], (IN, OUT), dtype=jnp.float32) * IN ** (-0.5), 'W_k': jax.random.normal(ks[4], (IN, OUT), dtype=jnp.float32) * IN ** (-0.5), 'ln_g': jnp.ones((OUT,), dtype=jnp.float32), 'ln_b': jnp.zeros((OUT,), dtype=jnp.float32)}
    _L0_gnn_all = _L0_gnn_setup()
    _L0_gnn_in = {k: v for k, v in _L0_gnn_all.items() if k in ('W_lin', 'b_lin', 'W_q', 'W_k', 'ln_g', 'ln_b')}
    del _L0_gnn_all

    def _L0_ffn_setup():
        import jax, jax.numpy as jnp
        import numpy as np
        B, S, D, E, H, K = (4, 2048, 128, 8, 256, 2)
        key = jax.random.key(seed)
        ks = jax.random.split(key, 6)
        x = jax.random.normal(ks[0], (B, S, D), jnp.float32)
        Wg = jax.random.normal(ks[1], (D, E), jnp.float32) * 0.02
        bg = jnp.zeros((E,), jnp.float32)
        W1 = jax.random.normal(ks[2], (E, D, H), jnp.float32) * 0.02
        b1 = jnp.zeros((E, H), jnp.float32)
        W2 = jax.random.normal(ks[3], (E, H, D), jnp.float32) * 0.02
        b2 = jnp.zeros((E, D), jnp.float32)
        return {'x': x, 'Wg': Wg, 'bg': bg, 'W1': W1, 'b1': b1, 'W2': W2, 'b2': b2}
    _L0_ffn_all = _L0_ffn_setup()
    _L0_ffn_in = {k: v for k, v in _L0_ffn_all.items() if k in ('Wg', 'bg', 'W1', 'b1', 'W2', 'b2')}
    del _L0_ffn_all

    def _L1_gnn_setup():
        import jax, jax.numpy as jnp
        import numpy as np
        B, N, D = (2, 2048, 128)
        key = jax.random.key(seed)
        ks = jax.random.split(key, 6)
        return {'hidden': jax.random.normal(ks[0], (B, N, D), dtype=jnp.float32), 'mask': jax.random.uniform(ks[1], (B, N, N), dtype=jnp.float32), 'W_w': jax.random.normal(ks[2], (D, D), dtype=jnp.float32) * 0.05, 'W_b': jax.random.normal(ks[3], (D,), dtype=jnp.float32) * 0.05, 'a_w': jax.random.normal(ks[4], (2 * D,), dtype=jnp.float32) * 0.05, 'a_b': jax.random.normal(ks[5], (1,), dtype=jnp.float32) * 0.05}
    _L1_gnn_all = _L1_gnn_setup()
    _L1_gnn_in = {k: v for k, v in _L1_gnn_all.items() if k in ('W_w', 'W_b', 'a_w', 'a_b')}
    del _L1_gnn_all

    def _L1_ffn_setup():
        import math
        import jax, jax.numpy as jnp
        import numpy as np
        CAPACITY_FACTOR = 1.25
        TOP_K = 2
        LN_EPS = 1e-05

        def _layer_norm(x, gamma, beta):
            mu = jnp.mean(x, axis=-1, keepdims=True)
            var = jnp.var(x, axis=-1, keepdims=True)
            return (x - mu) * jax.lax.rsqrt(var + LN_EPS) * gamma + beta
        key = jax.random.key(seed)
        ks = jax.random.split(key, 4)
        B, S, D, F, E = (8, 2048, 128, 256, 8)
        x = jax.random.normal(ks[0], (B, S, D), dtype=jnp.float32)
        Wr = jax.random.normal(ks[1], (D, E), dtype=jnp.float32) / np.sqrt(D)
        br = jnp.zeros((E,), jnp.float32)
        W1 = jax.random.normal(ks[2], (E, D, F), dtype=jnp.float32) / np.sqrt(D)
        b1 = jnp.zeros((E, F), jnp.float32)
        W2 = jax.random.normal(ks[3], (E, F, D), dtype=jnp.float32) / np.sqrt(F)
        b2 = jnp.zeros((E, D), jnp.float32)
        gamma = jnp.ones((D,), jnp.float32)
        beta = jnp.zeros((D,), jnp.float32)
        return {'x': x, 'Wr': Wr, 'br': br, 'W1': W1, 'b1': b1, 'W2': W2, 'b2': b2, 'gamma': gamma, 'beta': beta}
    _L1_ffn_all = _L1_ffn_setup()
    _L1_ffn_in = {k: v for k, v in _L1_ffn_all.items() if k in ('Wr', 'br', 'W1', 'b1', 'W2', 'b2', 'gamma', 'beta')}
    del _L1_ffn_all
    return {'x': x, 'adj': adj, 'L0_gnn_W_lin': _L0_gnn_in['W_lin'], 'L0_gnn_b_lin': _L0_gnn_in['b_lin'], 'L0_gnn_W_q': _L0_gnn_in['W_q'], 'L0_gnn_W_k': _L0_gnn_in['W_k'], 'L0_gnn_ln_g': _L0_gnn_in['ln_g'], 'L0_gnn_ln_b': _L0_gnn_in['ln_b'], 'L0_ffn_Wg': _L0_ffn_in['Wg'], 'L0_ffn_bg': _L0_ffn_in['bg'], 'L0_ffn_W1': _L0_ffn_in['W1'], 'L0_ffn_b1': _L0_ffn_in['b1'], 'L0_ffn_W2': _L0_ffn_in['W2'], 'L0_ffn_b2': _L0_ffn_in['b2'], 'L1_gnn_W_w': _L1_gnn_in['W_w'], 'L1_gnn_W_b': _L1_gnn_in['W_b'], 'L1_gnn_a_w': _L1_gnn_in['a_w'], 'L1_gnn_a_b': _L1_gnn_in['a_b'], 'L1_ffn_Wr': _L1_ffn_in['Wr'], 'L1_ffn_br': _L1_ffn_in['br'], 'L1_ffn_W1': _L1_ffn_in['W1'], 'L1_ffn_b1': _L1_ffn_in['b1'], 'L1_ffn_W2': _L1_ffn_in['W2'], 'L1_ffn_b2': _L1_ffn_in['b2'], 'L1_ffn_gamma': _L1_ffn_in['gamma'], 'L1_ffn_beta': _L1_ffn_in['beta']}

def reference(x, adj, L0_gnn_W_lin, L0_gnn_b_lin, L0_gnn_W_q, L0_gnn_W_k, L0_gnn_ln_g, L0_gnn_ln_b, L0_ffn_Wg, L0_ffn_bg, L0_ffn_W1, L0_ffn_b1, L0_ffn_W2, L0_ffn_b2, L1_gnn_W_w, L1_gnn_W_b, L1_gnn_a_w, L1_gnn_a_b, L1_ffn_Wr, L1_ffn_br, L1_ffn_W1, L1_ffn_b1, L1_ffn_W2, L1_ffn_b2, L1_ffn_gamma, L1_ffn_beta):
    import jax
    import jax.numpy as jnp

    def _L0_gnn_ref(node_feats, adj_matrix, W_lin, b_lin, W_q, W_k, ln_g, ln_b):
        import jax, jax.numpy as jnp
        import numpy as np
        H = 4
        LN_EPS = 1e-05

        def _heads(x, B, N):
            return x.reshape(B, N, H, -1).transpose(0, 2, 1, 3)
        B, N, _ = node_feats.shape
        out_dim = W_lin.shape[1]
        hd = out_dim // H
        scale = hd ** (-0.5)
        lrelu = lambda z: jax.nn.leaky_relu(z, 0.01)
        X = _heads(lrelu(node_feats @ W_lin + b_lin), B, N)
        q = _heads(lrelu(node_feats @ W_q), B, N)
        k = _heads(lrelu(node_feats @ W_k), B, N)
        att = jax.nn.sigmoid(jnp.einsum('bhxd,bhyd->bhxy', q, k) * scale)
        adj_h = adj_matrix[:, None] * att
        deg = jnp.sum(adj_h, axis=-1)
        dis = jnp.where(deg > 0, deg ** (-0.5), 0.0)
        A = dis[..., :, None] * adj_h * dis[..., None, :]
        Y = jnp.einsum('bhxy,bhyd->bhxd', A, X)
        Y = Y.transpose(0, 2, 1, 3).reshape(B, N, out_dim)
        mu = jnp.mean(Y, axis=-1, keepdims=True)
        var = jnp.mean((Y - mu) ** 2, axis=-1, keepdims=True)
        return (Y - mu) * jax.lax.rsqrt(var + LN_EPS) * ln_g + ln_b

    def _L0_ffn_ref(x, Wg, bg, W1, b1, W2, b2):
        import jax, jax.numpy as jnp
        import numpy as np
        B, S, D, E, H, K = (4, 2048, 128, 8, 256, 2)
        Bv, Sv, Dv = x.shape
        gate_scores = x @ Wg + bg
        _, idx = jax.lax.top_k(gate_scores, K)
        mask = jax.nn.one_hot(idx, E, dtype=x.dtype).sum(axis=-2)
        xf = x.reshape(-1, Dv)
        mf = mask.reshape(-1, E)
        h = jax.nn.gelu(jnp.einsum('td,edh->teh', xf, W1) + b1[None], approximate=False)
        y = jnp.einsum('teh,ehd->ted', h, W2) + b2[None]
        out = jnp.einsum('ted,te->td', y, mf)
        return out.reshape(Bv, Sv, Dv)

    def _L1_gnn_ref(hidden, mask, W_w, W_b, a_w, a_b):
        import jax, jax.numpy as jnp
        import numpy as np
        B, N, D = (2, 2048, 128)
        h = jnp.einsum('bnd,ed->bne', hidden, W_w) + W_b
        Dh = h.shape[-1]
        a1, a2 = (a_w[:Dh], a_w[Dh:])
        e = h @ a1
        f = h @ a2
        logits = e[:, :, None] + f[:, None, :] + a_b[0]
        u = mask * jnp.exp(logits)
        a = u / jnp.sum(u, axis=2, keepdims=True)
        h_prime = jnp.einsum('bnm,bmd->bnd', a, h)
        return h_prime

    def _L1_ffn_ref(x, Wr, br, W1, b1, W2, b2, gamma, beta):
        import math
        import jax, jax.numpy as jnp
        import numpy as np
        CAPACITY_FACTOR = 1.25
        TOP_K = 2
        LN_EPS = 1e-05

        def _layer_norm(x, gamma, beta):
            mu = jnp.mean(x, axis=-1, keepdims=True)
            var = jnp.var(x, axis=-1, keepdims=True)
            return (x - mu) * jax.lax.rsqrt(var + LN_EPS) * gamma + beta
        B, S, D = x.shape
        E = Wr.shape[1]
        N = B * S
        K = TOP_K
        logits = jnp.mean(x, axis=1) @ Wr + br
        routing_weights = jax.nn.softmax(logits, axis=-1)
        capacity = float(math.ceil(N * CAPACITY_FACTOR / E))
        expected_loads = routing_weights.sum(axis=0) * (N / B)
        scale = jnp.where(expected_loads > capacity, capacity / expected_loads, 1.0)
        routing_weights = jax.nn.softmax(routing_weights * scale, axis=-1)
        rw_tok = jnp.broadcast_to(routing_weights[:, None, :], (B, S, E)).reshape(N, E)
        top_w, top_i = jax.lax.top_k(rw_tok, K)
        top_w = jax.nn.softmax(top_w, axis=-1)
        xf = x.reshape(N, D)
        h = jax.nn.gelu(jnp.einsum('nd,edf->enf', xf, W1) + b1[:, None, :], approximate=False)
        y = jnp.einsum('enf,efd->end', h, W2) + b2[:, None, :]
        w_dense = jnp.zeros((N, E), x.dtype).at[jnp.arange(N)[:, None], top_i].add(top_w)
        out = jnp.einsum('ne,end->nd', w_dense, y).reshape(B, S, D)
        out = _layer_norm(out + x, gamma, beta)
        return out
    x = x + _L0_gnn_ref(_layernorm(x, axis=-1), adj, L0_gnn_W_lin, L0_gnn_b_lin, L0_gnn_W_q, L0_gnn_W_k, L0_gnn_ln_g, L0_gnn_ln_b)
    x = x + _L0_ffn_ref(_layernorm(x, axis=-1), L0_ffn_Wg, L0_ffn_bg, L0_ffn_W1, L0_ffn_b1, L0_ffn_W2, L0_ffn_b2)
    x = x + _L1_gnn_ref(_layernorm(x, axis=-1), adj, L1_gnn_W_w, L1_gnn_W_b, L1_gnn_a_w, L1_gnn_a_b)
    x = x + _L1_ffn_ref(_layernorm(x, axis=-1), L1_ffn_Wr, L1_ffn_br, L1_ffn_W1, L1_ffn_b1, L1_ffn_W2, L1_ffn_b2, L1_ffn_gamma, L1_ffn_beta)
    return x

_drawn_inputs = setup_inputs


def setup_inputs(seed=0):
    import zlib

    import numpy as np

    out = dict(_drawn_inputs(seed))
    spreads = {'L0_gnn_b_lin': (0.0, 0.1),
     'L0_gnn_ln_g': (1.0, 0.2),
     'L0_gnn_ln_b': (0.0, 0.1),
     'L0_ffn_bg': (0.0, 0.1),
     'L0_ffn_b1': (0.0, 0.1),
     'L0_ffn_b2': (0.0, 0.1),
     'L1_ffn_br': (0.0, 0.1),
     'L1_ffn_b1': (0.0, 0.459),
     'L1_ffn_b2': (0.0, 0.305),
     'L1_ffn_gamma': (1.0, 0.2),
     'L1_ffn_beta': (0.0, 0.1)}
    factors = {}
    for name, (base, spread) in spreads.items():
        noise = np.random.default_rng([zlib.crc32(name.encode()), seed]).standard_normal(out[name].shape)
        drawn = base * np.exp(spread * noise) if base else spread * noise
        out[name] = jnp.asarray(drawn.astype(out[name].dtype))
    for name, factor in factors.items():
        out[name] = (out[name] * factor).astype(out[name].dtype)
    return out
```

```python
from contextlib import ExitStack

import concourse.bass as bass
from concourse import mybir

F32 = mybir.dt.float32
I32 = mybir.dt.int32
ALU = mybir.AluOpType
ACT = mybir.ActivationFunctionType
AX_X = mybir.AxisListType.X

P = 128
D = 128
NB = 32
NN = 256
HEADS = 4
HD = D // HEADS
GB = 4
NG = NB // GB
GT = GB * NN // P
NT = NB * NN // P
GTOK = GB * NN
NE = 8
HID = 256
FC = HID // P
TOPK = 2
EPS = 1e-5
BANK = 512
DEG_MIN = 2.0 ** -64
RSQRT_MAGIC = float(0x5F3759DF)


class Chain:

    def __init__(self, engine, sem, per):
        self.engine, self.sem, self.per, self.base, self.k = engine, sem, per, 0, 0

    def body(self, n):
        assert self.k in (0, self.per), (self.k, self.per)
        self.base, self.k = n * self.per, 0

    def mark(self, ins):
        self.k += 1
        ins.then_inc(self.sem, 1)

    def settle(self):
        self.engine.wait_ge(self.sem, self.base + self.k)

    def link(self, ins):
        self.mark(ins)
        self.settle()


def build_program(nc, I, out):
    with ExitStack() as ctx:
        def sb(name, shape, dt=F32):
            return ctx.enter_context(nc.sbuf_tensor(name, shape, dt))

        def sem(name):
            return ctx.enter_context(nc.semaphore(name))

        x_dram = I["x"].rearrange("(g b) (t p) d -> g p (b t) d", b=GB, p=P)
        adj_dram = I["adj"].rearrange("(g b) (c p) y -> g p (b c) y", b=GB, p=P)
        out_dram = out.rearrange("(g b) (t p) d -> g p (b t) d", b=GB, p=P)
        adjT_dram = nc.dram_tensor("adjT_scratch", (NG, P, GB * 2 * NN), F32).ap()

        ident = sb("ident", [P, P])
        ones = sb("ones", [P, P])
        xres = sb("xres", [P, NT, D])

        f0_wg = sb("f0_wg", [P, NE])
        f0_bg = sb("f0_bg", [P, NE])
        f0_w1 = sb("f0_w1", [P, NE, HID])
        f0_b1 = sb("f0_b1", [P, NE, FC])
        f0_w2 = sb("f0_w2", [P, NE, FC, D])
        f0_b2 = sb("f0_b2", [NE, D])
        s_w2 = sem("s_w2")
        rank8 = sb("rank8", [P, NE])

        stats = sb("stats", [P, GT, 6])
        msum = sb("msum", [P, GT])
        mdiff = sb("mdiff", [P, GT])
        sqsum = sb("sqsum", [P, GT])
        mean = sb("mean", [P, GT])
        veps = sb("veps", [P, GT])
        rstd = sb("rstd", [P, GT])
        newt = sb("newt", [P, GT])

        psum = ctx.enter_context(nc.psum_tensor("psum", [P, 8, BANK], F32))

        s_const = sem("s_const")
        pool_token = sb("pool_token", [P, 1])
        act_token = sb("act_token", [P, 1])
        s_out = sem("s_out")

        def chained_layernorm(ch, src_of):
            for t in range(GT):
                ch.mark(nc.vector.bn_stats(stats[:, t, :], src_of(t)))
            ch.settle()
            mean_a, sq_a, mean_b, sq_b = (stats[:, :, i] for i in (1, 2, 4, 5))
            ch.mark(nc.vector.tensor_tensor(msum[:, :], mean_a, mean_b, ALU.add))
            ch.mark(nc.vector.tensor_tensor(mdiff[:, :], mean_a, mean_b, ALU.subtract))
            ch.mark(nc.vector.tensor_tensor(sqsum[:, :], sq_a, sq_b, ALU.add))
            ch.settle()
            ch.mark(nc.vector.tensor_scalar(mean[:, :], msum[:, :], 0.5, None, ALU.mult))
            ch.mark(nc.vector.scalar_tensor_tensor(mdiff[:, :], mdiff[:, :], 0.25, mdiff[:, :],
                                                   ALU.mult, ALU.mult))
            ch.mark(nc.vector.tensor_scalar(sqsum[:, :], sqsum[:, :], 1.0 / D, EPS, ALU.mult, ALU.add))
            ch.settle()
            ch.link(nc.vector.tensor_tensor(veps[:, :], sqsum[:, :], mdiff[:, :], ALU.add))
            ch.link(nc.vector.tensor_scalar(rstd[:, :].bitcast(I32), veps[:, :].bitcast(I32),
                                            -0.5, RSQRT_MAGIC, ALU.mult, ALU.add))
            for _ in range(3):
                ch.link(nc.vector.scalar_tensor_tensor(newt[:, :], rstd[:, :], -0.5, rstd[:, :],
                                                       ALU.mult, ALU.mult))
                ch.link(nc.vector.tensor_tensor(newt[:, :], newt[:, :], veps[:, :], ALU.mult))
                ch.link(nc.vector.scalar_tensor_tensor(rstd[:, :], newt[:, :], 1.5, rstd[:, :],
                                                       ALU.add, ALU.mult))

        LN_LINKS = GT + 6 + 2 + 9

        def tile_of_x(g, t):
            return xres[:, bass.ds(g * GT + t, 1), :].rearrange("p a d -> p (a d)")

        ph1 = ExitStack()
        ctx.push(ph1)

        def sb1(name, shape, dt=F32):
            return ph1.enter_context(nc.sbuf_tensor(name, shape, dt))

        w_k, w_q, w_lin = sb1("w_k", [P, D]), sb1("w_q", [P, D]), sb1("w_lin", [P, D])
        b_lin = sb1("b_lin", [P, 1])
        ln_g, ln_b = sb1("ln_g", [P, D]), sb1("ln_b", [P, D])
        adj_in = sb1("adj_in", [P, GT, NN])
        adjT = sb1("adjT", [P, GB, 2, NN])
        xh = sb1("xh", [P, GT, D])
        xhT = sb1("xhT", [P, GTOK])
        raw = sb1("raw", [P, 3, GTOK])
        kqxT = sb1("kqxT", [P, 3, GTOK])
        kheadT = sb1("kheadT", [P, HEADS, GTOK])
        att = sb1("att", [P, 2, 2, 2, NN])
        adj_h = sb1("adj_h", [P, GB, 2, 2, 2, NN])
        deg = sb1("deg", [P, GTOK])
        dis = sb1("dis", [P, GTOK])
        xs = sb1("xs", [P, GT, D])
        xsT = sb1("xsT", [P, GTOK])
        yT = sb1("yT", [P, NN])
        y_sb = sb1("y_sb", [P, GT, D])
        y_n = sb1("y_n", [P, GT, D])

        s_w1 = sem("s_w1")
        s_x = sem("s_x")
        s_adj = sem("s_adj")
        s_khead = sem("s_khead")
        s_adjT_out = sem("s_adjT_out")
        s_xhT_ps, s_adjT_ps, s_proj_ps = sem("s_xhT_ps"), sem("s_adjT_ps"), sem("s_proj_ps")
        s_score_ps, s_deg_ps = sem("s_score_ps"), sem("s_deg_ps")
        s_xs_ps, s_yT_ps, s_y_ps = sem("s_xs_ps"), sem("s_yT_ps"), sem("s_y_ps")
        s_xhT, s_adjT, s_raw, s_att = sem("s_xhT"), sem("s_adjT"), sem("s_raw"), sem("s_att")
        s_ln, s_dis, s_xs, s_y = sem("s_ln"), sem("s_dis"), sem("s_xs"), sem("s_y")
        s_xh, s_kqx, s_adjh, s_deg = sem("s_xh"), sem("s_kqx"), sem("s_adjh"), sem("s_deg")
        s_degpos, s_xsT, s_yT, s_yn = sem("s_degpos"), sem("s_xsT"), sem("s_yT"), sem("s_yn")
        s_chA, s_chB = sem("s_chA"), sem("s_chB")
        s_x1 = sem("s_x1")
        s_poolc = sem("s_poolc")

        two01 = psum[:, 0:2, :].rearrange("p a n -> p (a n)")
        two23 = psum[:, 2:4, :].rearrange("p a n -> p (a n)")
        deg_ps, xs_ps, yT_ps, y_ps = (psum[:, 4 + i, :] for i in range(4))

        def for_groups(engine, body):
            body(0, True, False)
            with engine.Fori(1, NG) as g:
                body(g, True, True)
            body(NG, False, True)

        def gnn0_sync(sp):
            for dst, name in ((w_k, "L0_gnn_W_k"), (w_q, "L0_gnn_W_q"), (w_lin, "L0_gnn_W_lin")):
                sp.dma_start(dst[:, :], I[name]).then_inc(s_w1, 16)
            sp.dma_start(b_lin[:, :], I["L0_gnn_b_lin"].rearrange("(p a) -> p a", a=1)).then_inc(s_w1, 16)
            for dst, name in ((ln_g, "L0_gnn_ln_g"), (ln_b, "L0_gnn_ln_b")):
                sp.dma_start(dst[:, :], I[name].rearrange("(a n) -> a n", a=1).to_broadcast((P, D)))\
                    .then_inc(s_w1, 16)
            sp.dma_start(xres[:, 0:GT, :], x_dram[0]).then_inc(s_x, 16)
            sp.dma_start(adj_in[:, :, :], adj_dram[0]).then_inc(s_adj, 16)
            load_weights(sp)

            def split_heads(g):
                sp.wait_ge(s_kqx, 3 * g + 1)
                for h in range(HEADS):
                    rows = slice(HD * h, HD * (h + 1))
                    sp.dma_start(kheadT[rows, h, :], kqxT[rows, 0, :]).then_inc(s_khead, 16)

            sp.wait_ge(s_const, 3)
            split_heads(0)
            with sp.Fori(1, NG) as g:
                sp.wait_ge(s_x, 16 * g)
                sp.dma_start(xres[:, bass.ds(g * GT, GT), :], x_dram[g]).then_inc(s_x, 16)
                sp.wait_ge(s_adjT_ps, GB * g)
                sp.wait_ge(s_adj, 16 * g)
                sp.dma_start(adj_in[:, :, :], adj_dram[g]).then_inc(s_adj, 16)
                sp.wait_ge(s_khead, 64 * g)
                sp.wait_ge(s_score_ps, 8 * g)
                split_heads(g)

        def gnn0_tensor(pe):
            pe.wait_ge(s_const, 3)
            pe.wait_ge(s_w1, 6 * 16)

            def body(g, a, b):
                if a:
                    pe.wait_ge(s_xh, g + 1)
                    if b:
                        pe.wait_ge(s_att, 8 * g)
                    for t in range(GT):
                        ins = nc.tensor.transpose(two01[:, t * P:(t + 1) * P], xh[:, t, :], ident[:, :])
                    ins.then_inc(s_xhT_ps, 1)

                    def transpose_adj(j):
                        if j == 0:
                            pe.wait_ge(s_adj, 16 * (g + 1))
                            if b:
                                pe.wait_ge(s_deg, GB * g)
                        bank = psum[:, 4 + j, :]
                        for c in range(2):
                            for r in range(2):
                                ins = nc.tensor.transpose(
                                    bank[:, c * NN + r * P:c * NN + (r + 1) * P],
                                    adj_in[:, 2 * j + r, c * P:(c + 1) * P], ident[:, :])
                        ins.then_inc(s_adjT_ps, 1)

                    def project(n, w, dst):
                        for c in range(2):
                            ins = nc.tensor.matmul(dst[:, c * BANK:(c + 1) * BANK], w[:, :],
                                                   xhT[:, c * BANK:(c + 1) * BANK], start=True, stop=True)
                        ins.then_inc(s_proj_ps, 1)

                    transpose_adj(0)
                    transpose_adj(1)
                    pe.wait_ge(s_xhT, g + 1)
                    project(0, w_k, two23)
                    project(1, w_q, two01)
                    transpose_adj(2)
                    transpose_adj(3)
                    pe.wait_ge(s_raw, 3 * g + 1)
                    project(2, w_lin, two23)

                def degrees(j):
                    pe.wait_ge(s_adjh, 8 * g + 2 * j + 2)
                    if j == 0:
                        pe.wait_ge(s_adjT, GB * g + 1)
                    else:
                        pe.wait_ge(s_deg, GB * g + j)
                    for c in range(2):
                        for h in range(HEADS):
                            ins = nc.tensor.matmul(deg_ps[HD * h:HD * (h + 1), 0:NN], ones[:, 0:HD],
                                                   adj_h[:, j, h // 2, h % 2, c, :], start=(c == 0), stop=(c == 1))
                    ins.then_inc(s_deg_ps, 1)

                def scores(j, u):
                    if j == 0 and u == 0:
                        pe.wait_ge(s_khead, 64 * g + 64)
                        pe.wait_ge(s_kqx, 3 * g + 2)
                    if j == 0:
                        pe.wait_ge(s_raw, 3 * g + 2 + u)
                    else:
                        pe.wait_ge(s_att, 8 * g + 2 * j - 1 + u)
                    for c in range(2):
                        for h in (2 * u, 2 * u + 1):
                            ins = nc.tensor.matmul(
                                psum[:, h, c * NN:(c + 1) * NN],
                                kheadT[:, h, j * NN + c * P:j * NN + (c + 1) * P],
                                kqxT[:, 1, j * NN:(j + 1) * NN], start=True, stop=True)
                    ins.then_inc(s_score_ps, 1)

                for j in range(GB):
                    n = GB * (g - 1) + j
                    if a:
                        scores(j, 0)
                    if b:
                        if j == 0:
                            pe.wait_ge(s_xsT, g)
                            if a:
                                pe.wait_ge(s_adjT, GB * g + 4)
                        else:
                            pe.wait_ge(s_xs, n)
                        for t in range(2):
                            ins = nc.tensor.transpose(xs_ps[:, t * P:(t + 1) * P],
                                                      xsT[:, j * NN + t * P:j * NN + (t + 1) * P], ident[:, :])
                        ins.then_inc(s_xs_ps, 1)
                    if a:
                        scores(j, 1)
                    if b:
                        pe.wait_ge(s_xs, n + 1)
                        if j > 0:
                            pe.wait_ge(s_yT, n)
                        for c in range(2):
                            for h in range(HEADS):
                                ins = nc.tensor.matmul(yT_ps[HD * h:HD * (h + 1), 0:NN],
                                                       xs[:, 2 * j + c, HD * h:HD * (h + 1)],
                                                       adj_h[:, j, h // 2, h % 2, c, :], start=(c == 0), stop=(c == 1))
                        ins.then_inc(s_yT_ps, 1)
                    if a and j > 0:
                        degrees(j - 1)
                    if b:
                        pe.wait_ge(s_yT, n + 1)
                        if j > 0:
                            pe.wait_ge(s_y, n)
                        for t in range(2):
                            ins = nc.tensor.transpose(y_ps[:, t * P:(t + 1) * P],
                                                      yT[:, t * P:(t + 1) * P], ident[:, :])
                        ins.then_inc(s_y_ps, 1)
                if a:
                    degrees(GB - 1)
                if b:
                    pe.wait_ge(s_y, GB * g)

            for_groups(pe, body)

        def gnn0_scalar(act):
            act.wait_ge(s_w1, 6 * 16)
            act.wait_ge(s_const, 3)

            def body(g, a, b):
                def copy_adj(j):
                    act.wait_ge(s_adjT_ps, GB * g + j + 1)
                    nc.scalar.activation(adjT[:, j, :, :].rearrange("p c n -> p (c n)"),
                                         psum[:, 4 + j, :], ACT.Copy).then_inc(s_adjT, 1)

                def copy_projection(n, src):
                    act.wait_ge(s_proj_ps, 3 * g + n + 1)
                    if n < 2:
                        nc.scalar.activation(raw[:, n, :], src, ACT.Copy).then_inc(s_raw, 1)
                    else:
                        nc.scalar.activation(raw[:, n, :], src, ACT.Identity, bias=b_lin[:, :])\
                            .then_inc(s_raw, 1)

                if a:
                    act.wait_ge(s_xhT_ps, g + 1)
                    nc.scalar.activation(xhT[:, :], two01, ACT.Copy).then_inc(s_xhT, 1)
                    if b:
                        act.wait_ge(s_kqx, 3 * g)
                    copy_projection(0, two23)
                    copy_projection(1, two01)
                if b:
                    act.wait_ge(s_degpos, g)
                    nc.scalar.activation(dis[:, :], dis[:, :], ACT.Ln).then_inc(s_ln, 1)
                    act.wait_ge(s_ln, g)
                    nc.scalar.activation(dis[:, :], dis[:, :], ACT.Exp, scale=-0.5).then_inc(s_dis, 1)
                if a:
                    copy_projection(2, two23)
                    if b:
                        act.wait_ge(s_adjh, 8 * g)
                        act.wait_ge(s_adjT_out, 16 * g)
                    for j in range(GB):
                        copy_adj(j)
                    act.wait_ge(s_adjT, GB * g + GB)
                    act.dma_start(adjT_dram[g], adjT[:, :, :, :].rearrange("p b c n -> p (b c n)"))\
                        .then_inc(s_adjT_out, 16)

                def copy_y(j):
                    n = GB * (g - 1) + j
                    act.wait_ge(s_y_ps, n + 1)
                    nc.scalar.activation(y_sb[:, 2 * j:2 * j + 2, :].rearrange("p t d -> p (t d)"),
                                         y_ps[:, 0:NN], ACT.Copy).then_inc(s_y, 1)

                def sigmoid(j, u):
                    act.wait_ge(s_score_ps, 8 * g + 2 * j + u + 1)
                    if b or j > 0:
                        act.wait_ge(s_adjh, 8 * g + 2 * j - 1 + u)
                    nc.scalar.activation(att[:, u, :, :, :].rearrange("p h c n -> p (h c n)"),
                                         (two01, two23)[u], ACT.Sigmoid, scale=float(HD) ** -0.5)\
                        .then_inc(s_att, 1)

                for j in range(GB):
                    if a:
                        sigmoid(j, 0)
                    if b:
                        act.wait_ge(s_xs_ps, GB * (g - 1) + j + 1)
                        nc.scalar.activation(xs[:, 2 * j:2 * j + 2, :].rearrange("p t d -> p (t d)"),
                                             xs_ps[:, 0:NN], ACT.Copy).then_inc(s_xs, 1)
                        if j > 0:
                            copy_y(j - 1)
                    if a:
                        sigmoid(j, 1)
                if b:
                    copy_y(GB - 1)

            for_groups(act, body)

        LN0_LINKS = LN_LINKS
        CHB = 1 + LN_LINKS

        def gnn0_vector(dve):
            chA = Chain(dve, s_chA, LN0_LINKS)
            chB = Chain(dve, s_chB, CHB)

            def stats_in(g):
                chA.body(g)
                dve.wait_ge(s_x, 16 * (g + 1))
                chained_layernorm(chA, lambda t: tile_of_x(g, t))

            def normalise_in(g):
                for t in range(GT):
                    ins = nc.vector.tensor_scalar(xh[:, t, :], tile_of_x(g, t), mean[:, t:t + 1],
                                                  rstd[:, t:t + 1], ALU.subtract, ALU.mult)
                ins.then_inc(s_xh, 1)

            def leaky(g, n):
                dve.wait_ge(s_raw, 3 * g + n + 1)
                nc.vector.scalar_tensor_tensor(kqxT[:, n, :], raw[:, n, :], 0.01, raw[:, n, :],
                                               ALU.mult, ALU.max).then_inc(s_kqx, 1)

            def body(g, a, b, more=True):
                if b:
                    chB.body(g - 1)
                    dve.wait_ge(s_dis, g)
                    chB.link(nc.vector.scalar_tensor_tensor(dis[:, :], deg[:, :], 0.0, dis[:, :],
                                                            ALU.is_gt, ALU.mult))
                    nc.vector.tensor_tensor(xsT[:, :], kqxT[:, 2, :], dis[:, :], ALU.mult).then_inc(s_xsT, 1)
                    if a:
                        dve.wait_ge(s_xsT, g)
                if a:
                    leaky(g, 2)
                if a and more:
                    stats_in(g + 1)
                    dve.wait_ge(s_xhT_ps, g + 1)
                    normalise_in(g + 1)

                def weigh(j, c):
                    dve.wait_ge(s_att, 8 * g + 2 * j + c + 1)
                    if j == 0 and c == 0:
                        dve.wait_ge(s_adjT, GB * g + GB)
                    if b and c == 0:
                        dve.wait_ge(s_yT_ps, GB * (g - 1) + j + 1)
                    nc.vector.tensor_tensor(
                        adj_h[:, j, c, :, :, :].rearrange("p h c n -> p h (c n)"),
                        att[:, c, :, :, :].rearrange("p h c n -> p h (c n)"),
                        adjT[:, j, :, :].rearrange("p c n -> p (c n)").unsqueeze(1).to_broadcast((P, 2, 2 * NN)),
                        ALU.mult).then_inc(s_adjh, 1)

                def degrees(j):
                    dve.wait_ge(s_deg_ps, GB * g + j + 1)
                    if j == 0 and b:
                        dve.wait_ge(s_xsT, g)
                    nc.vector.tensor_copy(deg[:, j * NN:(j + 1) * NN], deg_ps[:, 0:NN]).then_inc(s_deg, 1)

                for j in range(GB):
                    if b:
                        n = GB * (g - 1) + j
                        dve.wait_ge(s_yT_ps, n + 1)
                        if j > 0:
                            dve.wait_ge(s_y_ps, n)
                        nc.vector.tensor_tensor(yT[:, :], yT_ps[:, 0:NN], dis[:, j * NN:(j + 1) * NN],
                                                ALU.mult).then_inc(s_yT, 1)
                    if a:
                        weigh(j, 0)
                        weigh(j, 1)
                        if j > 0:
                            degrees(j - 1)
                if a:
                    degrees(GB - 1)
                    if b:
                        dve.wait_ge(s_yT, GB * g)
                    dve.wait_ge(s_deg, GB * g + GB)
                    nc.vector.tensor_scalar(dis[:, :], deg[:, :], DEG_MIN, None, ALU.max).then_inc(s_degpos, 1)
                if b:
                    dve.wait_ge(s_y, GB * g)
                    chained_layernorm(chB, lambda t: y_sb[:, t, :])
                if a and more:
                    dve.wait_ge(s_khead, 64 * g + 64)
                    leaky(g + 1, 0)
                    leaky(g + 1, 1)
                if b:
                    dve.wait_ge(s_x1, g)
                    for t in range(GT):
                        ins = nc.vector.tensor_scalar(y_n[:, t, :], y_sb[:, t, :], mean[:, t:t + 1],
                                                      rstd[:, t:t + 1], ALU.subtract, ALU.mult)
                    ins.then_inc(s_yn, 1)

            stats_in(0)
            normalise_in(0)
            leaky(0, 0)
            leaky(0, 1)
            body(0, True, False)
            with dve.Fori(1, NG - 1) as g:
                body(g, True, True)
            body(NG - 1, True, True, more=False)
            body(NG, False, True)

        def gnn0_gpsimd(pool):
            nc.gpsimd.memset(y_n[:, :, :], 0.0).then_inc(s_x1, 1)
            pool.wait_ge(s_w1, 6 * 16)
            with pool.Fori(1, NG + 1) as g:
                pool.wait_ge(s_yn, g)
                nc.gpsimd.tensor_tensor(y_n[:, :, :], y_n[:, :, :],
                                        ln_g[:, :].unsqueeze(1).to_broadcast((P, GT, D)), ALU.mult)\
                    .then_inc(s_poolc, 1)
                pool.wait_ge(s_poolc, 2 * g)
                nc.gpsimd.tensor_tensor(y_n[:, :, :], y_n[:, :, :],
                                        ln_b[:, :].unsqueeze(1).to_broadcast((P, GT, D)), ALU.add)\
                    .then_inc(s_poolc, 1)
                pool.wait_ge(s_poolc, 2 * g + 1)
                xg = xres[:, bass.ds((g - 1) * GT, GT), :]
                nc.gpsimd.tensor_tensor(xg, y_n[:, :, :], xg, ALU.add).then_inc(s_x1, 1)

        s_ph1 = s_x1
        ph1.close()

        def load_weights(sp):
            sp.dma_start(f0_wg[:, :], I["L0_ffn_Wg"]).then_inc(s_w2, 16)
            sp.dma_start(f0_bg[:, :], I["L0_ffn_bg"].rearrange("(a n) -> a n", a=1).to_broadcast((P, NE)))\
                .then_inc(s_w2, 16)
            sp.dma_start(f0_w1[:, :, :], I["L0_ffn_W1"].rearrange("e d h -> d e h")).then_inc(s_w2, 16)
            sp.dma_start(f0_w2[:, :, :, :], I["L0_ffn_W2"].rearrange("e (c p) d -> p e c d", p=P))\
                .then_inc(s_w2, 16)
            with nc.allow_non_contiguous_dma(reason="2048 biases, one per partition"):
                for e in range(NE):
                    sp.dma_start(f0_b1[:, e, :], I["L0_ffn_b1"][e].rearrange("(c p) -> p c", p=P))\
                        .then_inc(s_w2, 16)
            sp.dma_start(f0_b2[:, :], I["L0_ffn_b2"]).then_inc(s_w2, 16)

        W2_LOADS = 16 * (5 + NE)

        def phase1_done(engine):
            engine.wait_ge(s_ph1, NG + 1)
            engine.wait_ge(s_adjT_out, 16 * NG)

        ph2 = ExitStack()
        ctx.push(ph2)

        def sb2(name, shape, dt=F32):
            return ph2.enter_context(nc.sbuf_tensor(name, shape, dt))

        xh1 = sb2("xh1", [P, GT, D])
        xh1T = sb2("xh1T", [P, GTOK])
        hT = sb2("hT", [P, 2, FC, BANK])
        gate = sb2("gate", [P, GT, NE])
        gate2 = sb2("gate2", [P, GT, NE])
        hot = sb2("hot", [P, TOPK, GT, NE])
        place = sb2("place", [P, GT, NE])
        gmax = sb2("gmax", [P, GT])
        emask = sb2("emask", [P, GT, NE])
        emaskT = sb2("emaskT", [NE, GTOK])
        acc = sb2("acc", [P, GT, D])
        s_xh1, s_xh1T_ps, s_xh1T = sem("s_xh1"), sem("s_xh1T_ps"), sem("s_xh1T")
        s_gate_ps, s_gate, s_mask, s_maskT_ps, s_maskT = (
            sem("s_gate_ps"), sem("s_gate"), sem("s_mask"), sem("s_maskT_ps"), sem("s_maskT"))
        s_b2_ps, s_acc0 = sem("s_b2_ps"), sem("s_acc0")
        s_h_ps, s_h, s_e_ps, s_acc = sem("s_h_ps"), sem("s_h"), sem("s_e_ps"), sem("s_acc")
        s_chC = sem("s_chC")
        s_x2 = sem("s_x2")
        STEPS2 = 2 * NE

        def top2(ch, sc, sc2, oh, pl, mx, rows, tiles, reverse):
            rev = reverse[0:rows, :].unsqueeze(1).to_broadcast((rows, tiles, NE))

            def wide(v):
                return v.unsqueeze(2).to_broadcast((rows, tiles, NE))

            for k in range(TOPK):
                src = (sc, sc2)[k]
                ch.link(nc.vector.tensor_reduce(mx, src, AX_X, ALU.max))
                ch.link(nc.vector.tensor_tensor(pl, src, wide(mx), ALU.is_equal))
                ch.link(nc.vector.tensor_tensor(pl, pl, rev, ALU.mult))
                ch.link(nc.vector.tensor_reduce(mx, pl, AX_X, ALU.max))
                ch.link(nc.vector.tensor_tensor(oh[k], pl, wide(mx), ALU.is_equal))
                if k == 0:
                    ch.link(nc.vector.scalar_tensor_tensor(sc2, oh[0], -3.0e38, sc, ALU.mult, ALU.add))

        TOP2_LINKS = 11

        def ffn0_tensor(pe):
            phase1_done(pe)
            pe.wait_ge(s_w2, W2_LOADS)

            with pe.Fori(0, NG) as g:
                pe.wait_ge(s_xh1, g + 1)
                for t in range(GT):
                    ins = nc.tensor.transpose(two01[:, t * P:(t + 1) * P], xh1[:, t, :], ident[:, :])
                ins.then_inc(s_xh1T_ps, 1)
                pe.wait_ge(s_xh1T, g + 1)
                for t in range(GT):
                    ins = nc.tensor.matmul(psum[:, 6, t * NE:(t + 1) * NE], xh1T[:, t * P:(t + 1) * P],
                                           f0_wg[:, :], start=True, stop=True)
                ins.then_inc(s_gate_ps, 1)
                pe.wait_ge(s_mask, g + 1)
                for t in range(GT):
                    ins = nc.tensor.transpose(two01[0:NE, t * P:(t + 1) * P], emask[:, t, :], ident[:, :])
                ins.then_inc(s_maskT_ps, 1)
                pe.wait_ge(s_maskT, g + 1)
                for t in range(GT):
                    ins = nc.tensor.matmul(two23[:, t * P:(t + 1) * P], emaskT[:, t * P:(t + 1) * P],
                                           f0_b2[:, :], start=True, stop=True)
                ins.then_inc(s_b2_ps, 1)

                def hidden(i):
                    e, half = divmod(i, 2)
                    if i == 1:
                        pe.wait_ge(s_acc0, g + 1)
                    elif i > 1:
                        pe.wait_ge(s_h, 2 * (STEPS2 * g + i - 1))
                    for c in range(FC):
                        ins = nc.tensor.matmul(psum[:, 2 * (i % 2) + c, :], f0_w1[:, e, c * P:(c + 1) * P],
                                               xh1T[:, half * BANK:(half + 1) * BANK], start=True, stop=True)
                        ins.then_inc(s_h_ps, 1)

                def output(i):
                    e, half = divmod(i, 2)
                    pe.wait_ge(s_h, 2 * (STEPS2 * g + i + 1))
                    if i > 1:
                        pe.wait_ge(s_acc, STEPS2 * g + i - 1)
                    for t in range(4):
                        for c in range(FC):
                            ins = nc.tensor.matmul(psum[:, 4 + i % 2, t * P:(t + 1) * P],
                                                   hT[:, i % 2, c, t * P:(t + 1) * P],
                                                   f0_w2[:, e, c, :], start=(c == 0), stop=(c == FC - 1))
                    ins.then_inc(s_e_ps, 1)

                hidden(0)
                for i in range(STEPS2):
                    if i + 1 < STEPS2:
                        hidden(i + 1)
                    output(i)
                pe.wait_ge(s_acc, STEPS2 * (g + 1))

        def ffn0_scalar(act):
            phase1_done(act)
            act.wait_ge(s_w2, W2_LOADS)
            with act.Fori(0, NG) as g:
                act.wait_ge(s_xh1T_ps, g + 1)
                nc.scalar.activation(xh1T[:, :], two01, ACT.Copy).then_inc(s_xh1T, 1)
                act.wait_ge(s_maskT_ps, g + 1)
                nc.scalar.activation(emaskT[:, :], two01[0:NE, :], ACT.Copy).then_inc(s_maskT, 1)
                for i in range(STEPS2):
                    for c in range(FC):
                        act.wait_ge(s_h_ps, 2 * (STEPS2 * g + i) + c + 1)
                        if c == 0 and i > 1:
                            act.wait_ge(s_e_ps, STEPS2 * g + i - 1)
                        nc.scalar.activation(hT[:, i % 2, c, :], psum[:, 2 * (i % 2) + c, :], ACT.Gelu,
                                             bias=f0_b1[:, i // 2, c:c + 1]).then_inc(s_h, 1)

        def ffn0_vector(dve):
            phase1_done(dve)
            dve.wait_ge(s_w2, W2_LOADS)
            ch = Chain(dve, s_chC, LN_LINKS + 1 + TOP2_LINKS)
            ch.body(0)
            with dve.Fori(0, NG) as g:
                ch.body(g)
                chained_layernorm(ch, lambda t: tile_of_x(g, t))
                for t in range(GT):
                    ins = nc.vector.tensor_scalar(xh1[:, t, :], tile_of_x(g, t), mean[:, t:t + 1],
                                                  rstd[:, t:t + 1], ALU.subtract, ALU.mult)
                ins.then_inc(s_xh1, 1)
                dve.wait_ge(s_gate_ps, g + 1)
                ch.link(nc.vector.tensor_tensor(
                    gate[:, :, :], psum[:, 6, 0:GT * NE].rearrange("p (t e) -> p t e", e=NE),
                    f0_bg[:, :].unsqueeze(1).to_broadcast((P, GT, NE)), ALU.add))
                top2(ch, gate[:, :, :], gate2[:, :, :], [hot[:, k, :, :] for k in range(TOPK)],
                     place[:, :, :], gmax[:, :], P, GT, rank8)
                nc.vector.tensor_tensor(emask[:, :, :], hot[:, 0, :, :], hot[:, 1, :, :], ALU.add)\
                    .then_inc(s_mask, 1)
                dve.wait_ge(s_mask, g + 1)
                dve.wait_ge(s_b2_ps, g + 1)
                xg = xres[:, bass.ds(g * GT, GT), :].rearrange("p t d -> p (t d)")
                nc.vector.tensor_tensor(acc[:, :, :].rearrange("p t d -> p (t d)"), two23, xg, ALU.add)\
                    .then_inc(s_acc0, 1)
                dve.wait_ge(s_acc0, g + 1)
                for i in range(STEPS2):
                    e, half = divmod(i, 2)
                    dve.wait_ge(s_e_ps, STEPS2 * g + i + 1)
                    if i > 1:
                        dve.wait_ge(s_acc, STEPS2 * g + i - 1)
                    for t in range(4):
                        tt = 4 * half + t
                        ins = nc.vector.scalar_tensor_tensor(
                            acc[:, tt, :], psum[:, 4 + i % 2, t * P:(t + 1) * P], emask[:, tt, e:e + 1],
                            acc[:, tt, :], ALU.mult, ALU.add)
                    ins.then_inc(s_acc, 1)
                dve.wait_ge(s_acc, STEPS2 * (g + 1))
                nc.vector.tensor_scalar(xres[:, bass.ds(g * GT, GT), :].rearrange("p t d -> p (t d)"),
                                        acc[:, :, :].rearrange("p t d -> p (t d)"), 1.0, None, ALU.mult)\
                    .then_inc(s_x2, 1)
                dve.wait_ge(s_x2, g + 1)

        ph2.close()

        xh3 = sb("xh3", [P, NT, D])
        xh3T = sb("xh3T", [P, NT * P])
        meanT = sb("meanT", [P, NB])
        f1_wr = sb("f1_wr", [P, NE])
        f1_br = sb("f1_br", [NB, NE])
        f1_w1 = sb("f1_w1", [P, NE * HID])
        f1_w2 = sb("f1_w2", [P, NE * FC * D])
        f1_b1 = sb("f1_b1", [P, NE, FC])
        f1_b2 = sb("f1_b2", [NE, D])
        gamma, beta = sb("gamma", [P, D]), sb("beta", [P, D])
        s_w4 = sem("s_w4")
        ph3 = ExitStack()
        ctx.push(ph3)

        def sb3(name, shape, dt=F32):
            return ph3.enter_context(nc.sbuf_tensor(name, shape, dt))

        ww = sb3("ww", [P, D])
        a_cols = sb3("a_cols", [P, 2])
        wb_col = sb3("wb_col", [P, 1])
        wb_row = sb3("wb_row", [P, D])
        wb_wide = sb3("wb_wide", [P, P])
        ab = sb3("ab", [P, 1])
        wh = sb3("wh", [P, D + 2])
        ef_bias = sb3("ef_bias", [P, 2])
        avg = sb3("avg", [P, 1])
        adjT2 = sb3("adjT2", [P, GB, 2, NN])
        xh2 = sb3("xh2", [P, GT, D])
        xh2T = sb3("xh2T", [P, GTOK])
        h_lin = sb3("h_lin", [P, GT, D])
        ef = sb3("ef", [P, GT, 2])
        expf = sb3("expf", [P, GT, 2])
        hf = sb3("hf", [P, GT, D + 1])
        den = sb3("den", [P, GT])
        h_new = sb3("h_new", [P, GT, D])
        xh3g = sb3("xh3g", [P, GT, D])

        s_w3, s_wwT_ps, s_init3 = sem("s_w3"), sem("s_wwT_ps"), sem("s_init3")
        s_adjT2 = sem("s_adjT2")
        s_xh2, s_xh2T_ps, s_xh2T, s_hl_ps = sem("s_xh2"), sem("s_xh2T_ps"), sem("s_xh2T"), sem("s_hl_ps")
        s_hlin, s_expf, s_hf, s_n_ps = sem("s_hlin"), sem("s_expf"), sem("s_hf"), sem("s_n_ps")
        s_hnew, s_x3, s_xh3g, s_xh3T_ps = sem("s_hnew"), sem("s_x3"), sem("s_xh3g"), sem("s_xh3T_ps")
        s_mean_ps, s_mean, s_xh3, s_xh3T = sem("s_mean_ps"), sem("s_mean"), sem("s_xh3"), sem("s_xh3T")
        s_chD, s_chE = sem("s_chD"), sem("s_chE")

        hl_ps = psum[:, 0:4, :].rearrange("p b (t n) -> p (b t) n", t=2)
        n_ps = psum[:, 4:8, :].rearrange("p b (t n) -> p (b t) n", t=2)
        two45 = psum[:, 4:6, :].rearrange("p a n -> p (a n)")

        def phase2_done(engine):
            engine.wait_ge(s_x2, NG)

        def gnn1_sync(sp):
            phase2_done(sp)
            sp.dma_start(ww[:, :], I["L1_gnn_W_w"]).then_inc(s_w3, 16)
            with nc.allow_non_contiguous_dma(reason="256 values, two per partition"):
                sp.dma_start(a_cols[:, :], I["L1_gnn_a_w"].rearrange("(k e) -> e k", k=2)).then_inc(s_w3, 16)
            sp.dma_start(wb_col[:, :], I["L1_gnn_W_b"].rearrange("(p a) -> p a", a=1)).then_inc(s_w3, 16)
            sp.dma_start(wb_row[:, :], I["L1_gnn_W_b"].rearrange("(a n) -> a n", a=1).to_broadcast((P, D)))\
                .then_inc(s_w3, 16)
            sp.dma_start(ab[:, :], I["L1_gnn_a_b"].rearrange("(a n) -> a n", a=1).to_broadcast((P, 1)))\
                .then_inc(s_w3, 16)
            sp.dma_start(adjT2[:, :, :, :].rearrange("p b c n -> p (b c n)"), adjT_dram[0])\
                .then_inc(s_adjT2, 16)
            load_weights4(sp)
            with sp.Fori(1, NG) as g:
                sp.wait_ge(s_adjT2, 16 * g)
                sp.wait_ge(s_n_ps, g)
                sp.dma_start(adjT2[:, :, :, :].rearrange("p b c n -> p (b c n)"), adjT_dram[g])\
                    .then_inc(s_adjT2, 16)

        W3_LOADS = 16 * 5

        def gnn1_tensor(pe):
            phase2_done(pe)
            pe.wait_ge(s_w3, W3_LOADS)
            pe.wait_ge(s_init3, 1)
            nc.tensor.transpose(psum[:, 0, 0:P], ww[:, :], ident[:, :]).then_inc(s_wwT_ps, 1)
            nc.tensor.matmul(psum[:, 1, 0:2], ww[:, :], a_cols[:, :], start=True, stop=True)\
                .then_inc(s_wwT_ps, 1)
            nc.tensor.matmul(psum[:, 2, 0:2], wb_wide[:, :], a_cols[:, :], start=True, stop=True)\
                .then_inc(s_wwT_ps, 1)
            pe.wait_ge(s_init3, 4)

            def body(g, a, b):
                if a:
                    pe.wait_ge(s_xh2, g + 1)
                    if b:
                        pe.wait_ge(s_hlin, 2 * g)
                    for t in range(GT):
                        ins = nc.tensor.transpose(two01[:, t * P:(t + 1) * P], xh2[:, t, :], ident[:, :])
                    ins.then_inc(s_xh2T_ps, 1)
                    pe.wait_ge(s_xh2T, g + 1)
                    for t in range(GT):
                        ins = nc.tensor.matmul(hl_ps[:, t, 0:D + 2], xh2T[:, t * P:(t + 1) * P], wh[:, :],
                                               start=True, stop=True)
                    ins.then_inc(s_hl_ps, 1)
                if b:
                    pe.wait_ge(s_xh3g, g)
                    for t in range(GT):
                        ins = nc.tensor.transpose(two45[:, t * P:(t + 1) * P], xh3g[:, t, :], ident[:, :])
                    ins.then_inc(s_xh3T_ps, 1)
                    for j in range(GB):
                        for r in range(2):
                            ins = nc.tensor.matmul(psum[:, 6, j:j + 1], xh3g[:, 2 * j + r, :], avg[:, :],
                                                   start=(r == 0), stop=(r == 1))
                    ins.then_inc(s_mean_ps, 1)
                if a:
                    pe.wait_ge(s_hf, 2 * g + 2)
                    pe.wait_ge(s_adjT2, 16 * (g + 1))
                    if b:
                        pe.wait_ge(s_mean, g + 1)
                        pe.wait_ge(s_xh3T, g)
                    for j in range(GB):
                        for r in range(2):
                            for c in range(2):
                                ins = nc.tensor.matmul(
                                    n_ps[:, 2 * j + r, 0:D + 1], adjT2[:, j, c, r * P:(r + 1) * P],
                                    hf[:, 2 * j + c, :], start=(c == 0), stop=(c == 1))
                    ins.then_inc(s_n_ps, 1)

            for_groups(pe, body)

        def gnn1_scalar(act):
            phase2_done(act)
            act.wait_ge(s_w3, W3_LOADS)
            nc.scalar.activation(act_token[:, :], ones[:, 0:1], ACT.Copy).then_inc(s_xh3, 1)

            def body(g, a, b):
                if a:
                    act.wait_ge(s_xh2T_ps, g + 1)
                    nc.scalar.activation(xh2T[:, :], two01, ACT.Copy).then_inc(s_xh2T, 1)
                if b:
                    act.wait_ge(s_xh3g, g)
                    nc.scalar.activation(xh3[:, bass.ds((g - 1) * GT, GT), :].rearrange("p t d -> p (t d)"),
                                         xh3g[:, :, :].rearrange("p t d -> p (t d)"), ACT.Copy)\
                        .then_inc(s_xh3, 1)
                    act.wait_ge(s_xh3T_ps, g)
                    nc.scalar.activation(xh3T[:, bass.ds((g - 1) * GTOK, GTOK)], two45, ACT.Copy)\
                        .then_inc(s_xh3T, 1)
                if a:
                    act.wait_ge(s_hlin, 2 * g + 2)
                    nc.scalar.activation(expf[:, :, :], ef[:, :, :], ACT.Exp).then_inc(s_expf, 1)

            for_groups(act, body)

        def gnn1_vector(dve):
            phase2_done(dve)
            dve.wait_ge(s_w3, W3_LOADS)
            nc.vector.memset(avg[:, :], 1.0 / NN).then_inc(s_mean, 1)
            nc.vector.tensor_scalar(wb_wide[:, :], ones[:, :], wb_col[:, 0:1], None, ALU.mult).then_inc(s_init3, 1)
            dve.wait_ge(s_wwT_ps, 3)
            nc.vector.tensor_copy(wh[:, 0:D], psum[:, 0, 0:P]).then_inc(s_init3, 1)
            nc.vector.tensor_copy(wh[:, D:D + 2], psum[:, 1, 0:2]).then_inc(s_init3, 1)
            nc.vector.tensor_copy(ef_bias[:, :], psum[:, 2, 0:2]).then_inc(s_init3, 1)
            dve.wait_ge(s_init3, 4)
            nc.vector.tensor_tensor(ef_bias[:, 0:1], ef_bias[:, 0:1], ab[:, :], ALU.add).then_inc(s_init3, 1)
            dve.wait_ge(s_init3, 5)
            chD = Chain(dve, s_chD, LN_LINKS)
            chE = Chain(dve, s_chE, LN_LINKS + 2)

            def body(g, a, b):
                if b:
                    chE.body(g - 1)
                    dve.wait_ge(s_n_ps, g)
                    chE.link(nc.vector.tensor_tensor(den[:, :], n_ps[:, :, D], expf[:, :, 0], ALU.mult))
                    chE.link(nc.vector.reciprocal(den[:, :], den[:, :]))
                    dve.wait_ge(s_x3, g)
                    for t in range(GT):
                        ins = nc.vector.tensor_scalar(h_new[:, t, :], n_ps[:, t, 0:D], expf[:, t, 0:1],
                                                      den[:, t:t + 1], ALU.mult, ALU.mult)
                    ins.then_inc(s_hnew, 1)
                if a:
                    chD.body(g)
                    chained_layernorm(chD, lambda t: tile_of_x(g, t))
                    if b:
                        dve.wait_ge(s_xh2T_ps, g)
                    for t in range(GT):
                        ins = nc.vector.tensor_scalar(xh2[:, t, :], tile_of_x(g, t), mean[:, t:t + 1],
                                                      rstd[:, t:t + 1], ALU.subtract, ALU.mult)
                    ins.then_inc(s_xh2, 1)
                    dve.wait_ge(s_xh2, g + 1)
                if b:
                    dve.wait_ge(s_x3, g + 1)
                    chained_layernorm(chE, lambda t: tile_of_x(g - 1, t))
                    dve.wait_ge(s_xh3, g)
                    dve.wait_ge(s_mean, g)
                    for t in range(GT):
                        ins = nc.vector.tensor_scalar(xh3g[:, t, :], tile_of_x(g - 1, t), mean[:, t:t + 1],
                                                      rstd[:, t:t + 1], ALU.subtract, ALU.mult)
                    ins.then_inc(s_xh3g, 1)
                    dve.wait_ge(s_xh3g, g)
                if a:
                    dve.wait_ge(s_hl_ps, g + 1)
                    nc.vector.tensor_tensor(h_lin[:, :, :], hl_ps[:, :, 0:D],
                                            wb_row[:, :].unsqueeze(1).to_broadcast((P, GT, D)), ALU.add)\
                        .then_inc(s_hlin, 1)
                    nc.vector.tensor_tensor(ef[:, :, :], hl_ps[:, :, D:D + 2],
                                            ef_bias[:, :].unsqueeze(1).to_broadcast((P, GT, 2)), ALU.add)\
                        .then_inc(s_hlin, 1)
                    dve.wait_ge(s_expf, g + 1)
                    nc.vector.tensor_tensor(hf[:, :, 0:D], h_lin[:, :, :],
                                            expf[:, :, 1:2].to_broadcast((P, GT, D)), ALU.mult).then_inc(s_hf, 1)
                    nc.vector.tensor_copy(hf[:, :, D], expf[:, :, 1]).then_inc(s_hf, 1)
                if b:
                    dve.wait_ge(s_mean_ps, g)
                    nc.vector.tensor_copy(meanT[:, bass.ds((g - 1) * GB, GB)], psum[:, 6, 0:GB]).then_inc(s_mean, 1)

            for_groups(dve, body)

        def gnn1_gpsimd(pool):
            phase2_done(pool)
            pool.wait_ge(s_w3, W3_LOADS)
            nc.gpsimd.memset(pool_token[:, :], 0.0).then_inc(s_x3, 1)
            with pool.Fori(1, NG + 1) as g:
                pool.wait_ge(s_hnew, g)
                xg = xres[:, bass.ds((g - 1) * GT, GT), :]
                nc.gpsimd.tensor_tensor(xg, h_new[:, :, :], xg, ALU.add).then_inc(s_x3, 1)

        ph3.close()

        def load_weights4(sp):
            sp.dma_start(f1_wr[:, :], I["L1_ffn_Wr"]).then_inc(s_w4, 16)
            sp.dma_start(f1_w1[:, :].rearrange("p (e h) -> p e h", e=NE), I["L1_ffn_W1"].rearrange("e d h -> d e h"))\
                .then_inc(s_w4, 16)
            sp.dma_start(f1_w2[:, :].rearrange("p (e c d) -> p e c d", e=NE, c=FC),
                         I["L1_ffn_W2"].rearrange("e (c p) d -> p e c d", p=P)).then_inc(s_w4, 16)
            with nc.allow_non_contiguous_dma(reason="2048 biases, one per partition"):
                for e in range(NE):
                    sp.dma_start(f1_b1[:, e, :], I["L1_ffn_b1"][e].rearrange("(c p) -> p c", p=P))\
                        .then_inc(s_w4, 16)
            sp.dma_start(f1_b2[:, :], I["L1_ffn_b2"]).then_inc(s_w4, 16)
            for dst, name, rows in ((f1_br, "L1_ffn_br", NB), (gamma, "L1_ffn_gamma", P), (beta, "L1_ffn_beta", P)):
                sp.dma_start(dst[:, :], I[name].rearrange("(a n) -> a n", a=1)
                             .to_broadcast((rows, dst.shape[1]))).then_inc(s_w4, 16)

        W4_LOADS = 16 * (3 + NE + 4)

        ph4 = ExitStack()
        ctx.push(ph4)

        def sb4(name, shape, dt=F32):
            return ph4.enter_context(nc.sbuf_tensor(name, shape, dt))

        logit = sb4("logit", [NB, NE])
        rexp = sb4("rexp", [NB, NE])
        rw = sb4("rw", [NB, NE])
        rw2 = sb4("rw2", [NB, 1, NE])
        rw2b = sb4("rw2b", [NB, 1, NE])
        rplace = sb4("rplace", [NB, 1, NE])
        scale = sb4("scale", [NB, NE])
        rmax = sb4("rmax", [NB, 1])
        rsum = sb4("rsum", [NB, 1])
        hot4 = sb4("hot4", [NB, TOPK, NE])
        first_row = sb4("first_row", [NB, NE])
        picked = sb4("picked", [NB, TOPK, NE])
        topw = sb4("topw", [NB, TOPK])
        topd = sb4("topd", [NB, 1])
        info = sb4("info", [NB, 2 * TOPK])
        wdense = sb4("wdense", [NB, NE])
        wd2 = sb4("wd2", [NB, NE])
        info_diag = sb4("info_diag", [NB, 2 * TOPK, NB])
        hot_diag = sb4("hot_diag", [NB, TOPK * NE, NB])
        wtok = sb4("wtok", [P, TOPK, NB])
        places = sb4("places", [1, TOPK, NB], I32)
        b1prod = sb4("b1prod", [P, TOPK * FC, NB, NE])
        b1sel = sb4("b1sel", [P, TOPK * FC, NB])
        wdT = sb4("wdT", [NE, NB])
        SLOTS4 = GB
        w1s = sb4("w1s", [P, SLOTS4, TOPK, HID])
        w2s = sb4("w2s", [P, SLOTS4, TOPK, FC * D])
        hT4 = sb4("hT4", [P, 2, TOPK, FC, NN])
        wb2 = sb4("wb2", [NE, GB, D])
        b2r = sb4("b2r", [P, GB, D])
        z = sb4("z", [P, GT, D])
        yout = sb4("yout", [P, GT, D])

        s_r_ps, s_r = sem("s_r_ps"), sem("s_r")
        s_rin, s_rexp = sem("s_rin"), sem("s_rexp")
        s_chR, s_chF = sem("s_chR"), sem("s_chF")
        s_info, s_wd, s_sel_ps, s_wtok, s_places, s_b1sel, s_wdT = (
            sem("s_info"), sem("s_wd"), sem("s_sel_ps"), sem("s_wtok"), sem("s_places"), sem("s_b1sel"), sem("s_wdT"))
        s_w1s, s_w2s, s_h4_ps, s_h4, s_o_ps, s_z = (
            sem("s_w1s"), sem("s_w2s"), sem("s_h4_ps"), sem("s_h4"), sem("s_o_ps"), sem("s_z"))
        s_wb2, s_b2r_ps, s_b2r, s_xb = sem("s_wb2"), sem("s_b2r_ps"), sem("s_b2r"), sem("s_xb")
        s_zs, s_yout = sem("s_zs"), sem("s_yout")

        CAPACITY = float(-(-NB * NN * 5 // (4 * NE)))

        def phase3_done(engine):
            engine.wait_ge(s_mean, NG + 1)
            engine.wait_ge(s_x3, NG + 1)
            engine.wait_ge(s_xh3, NG + 1)
            engine.wait_ge(s_xh3T, NG)
            engine.wait_ge(s_w4, W4_LOADS)

        def over_groups(engine, body):
            body(0, True, False)
            with engine.Fori(1, NG - 1) as g:
                body(g, False, False)
            body(NG - 1, False, True)

        def ffn1_sync(sp):
            with sp.Fori(0, NG) as g:
                sp.wait_ge(s_yout, g + 1)
                sp.dma_start(out_dram[g], yout[:, :, :]).then_inc(s_out, 16)
            sp.wait_ge(s_out, 16 * NG)

        def ffn1_tensor(pe):
            phase3_done(pe)
            nc.tensor.matmul(psum[0:NB, 0, 0:NE], meanT[:, :], f1_wr[:, :], start=True, stop=True)\
                .then_inc(s_r_ps, 1)
            pe.wait_ge(s_r, 1)
            nc.tensor.matmul(psum[0:NB, 1, 0:NE], ones[0:NB, 0:NB], rw[:, :], start=True, stop=True)\
                .then_inc(s_r_ps, 1)
            pe.wait_ge(s_info, 2)
            nc.tensor.matmul(psum[:, 2, 0:2 * TOPK * NB], ones[0:NB, :],
                             info_diag[:, :, :].rearrange("p k b -> p (k b)"), start=True, stop=True)\
                .then_inc(s_sel_ps, 1)
            nc.tensor.matmul(psum[:, 3, 0:TOPK * NE * NB], ones[0:NB, :],
                             hot_diag[:, :, :].rearrange("p k b -> p (k b)"), start=True, stop=True)\
                .then_inc(s_sel_ps, 1)
            pe.wait_ge(s_wd, 1)
            nc.tensor.transpose(psum[0:NE, 4, 0:NB], wdense[:, :], ident[0:NB, 0:NB]).then_inc(s_sel_ps, 1)

            def spread_b2(g):
                pe.wait_ge(s_wb2, g + 1)
                nc.tensor.matmul(psum[:, 6, 0:GB * D], ones[0:NE, :], wb2[:, :, :].rearrange("p b d -> p (b d)"),
                                 start=True, stop=True).then_inc(s_b2r_ps, 1)

            def hidden(g, j, first):
                n = GB * g + j
                pe.wait_ge(s_w1s, n + 1)
                if not (first and j < 2):
                    pe.wait_ge(s_h4, TOPK * FC * (n - 1))
                for k in range(TOPK):
                    for c in range(FC):
                        ins = nc.tensor.matmul(psum[:, 2 * (j % 2) + k, c * NN:(c + 1) * NN],
                                               w1s[:, j, k, c * P:(c + 1) * P],
                                               xh3T[:, bass.ds(g * GTOK + j * NN, NN)], start=True, stop=True)
                    ins.then_inc(s_h4_ps, 1)

            def output(g, j, first):
                n = GB * g + j
                pe.wait_ge(s_h4, TOPK * FC * (n + 1))
                pe.wait_ge(s_w2s, n + 1)
                if not (first and j < 2):
                    pe.wait_ge(s_z, n - 1)
                for r in range(2):
                    for i in range(TOPK * FC):
                        k, c = divmod(i, FC)
                        ins = nc.tensor.matmul(psum[:, 4 + j % 2, r * P:(r + 1) * P],
                                               hT4[:, j % 2, k, c, r * P:(r + 1) * P],
                                               w2s[:, j, k, c * D:(c + 1) * D],
                                               start=(i == 0), stop=(i == TOPK * FC - 1))
                ins.then_inc(s_o_ps, 1)

            pe.wait_ge(s_wdT, 1)
            pe.wait_ge(s_b1sel, 1)
            pe.wait_ge(s_wtok, 1)
            pe.wait_ge(s_places, 1)

            def body(g, first, last):
                spread_b2(g)
                for j in range(GB):
                    hidden(g, j, first)
                    if j > 0:
                        output(g, j - 1, first)
                    elif not first:
                        output(g - 1, GB - 1, False)
                if last:
                    output(g, GB - 1, False)

            over_groups(pe, body)

        def ffn1_scalar(act):
            phase3_done(act)
            for i, (src, dst) in enumerate(((logit[:, :], rexp[:, :]), (logit[:, :], rexp[:, :]),
                                            (topd[:, :], topd[:, :]))):
                act.wait_ge(s_rin, i + 1)
                nc.scalar.activation(dst, src, ACT.Exp).then_inc(s_rexp, 1)
            act.wait_ge(s_b1sel, 1)

            def body(g, first, last):
                act.wait_ge(s_b2r_ps, g + 1)
                if not first:
                    act.wait_ge(s_xb, g)
                nc.scalar.activation(b2r[:, :, :].rearrange("p b d -> p (b d)"), psum[:, 6, 0:GB * D], ACT.Copy)\
                    .then_inc(s_b2r, 1)
                for j in range(GB):
                    n = GB * g + j
                    for k in range(TOPK):
                        act.wait_ge(s_h4_ps, TOPK * n + k + 1)
                        if k == 0 and not (first and j < 2):
                            act.wait_ge(s_o_ps, n - 1)
                        for c in range(FC):
                            nc.scalar.activation(hT4[:, j % 2, k, c, :], psum[:, 2 * (j % 2) + k, c * NN:(c + 1) * NN],
                                                 ACT.Gelu, bias=b1sel[:, FC * k + c, bass.ds(g * GB + j, 1)])\
                                .then_inc(s_h4, 1)

            over_groups(act, body)

        LN4_LINKS = LN_LINKS + GT

        def ffn1_vector(dve):
            phase3_done(dve)
            ch = Chain(dve, s_chR, 10000)
            for e in range(NE):
                ch.mark(nc.vector.memset(first_row[:, e:e + 1], float(e * HID)))

            def softmax(values, dst):
                softmax.calls += 1
                ch.link(nc.vector.tensor_reduce(rmax[:, :], values, AX_X, ALU.max))
                nc.vector.tensor_scalar(logit[:, :], values, rmax[:, 0:1], None, ALU.subtract).then_inc(s_rin, 1)
                dve.wait_ge(s_rexp, softmax.calls)
                ch.link(nc.vector.tensor_reduce(rsum[:, :], rexp[:, :], AX_X, ALU.add))
                ch.link(nc.vector.reciprocal(rsum[:, :], rsum[:, :]))
                return nc.vector.tensor_scalar(dst, rexp[:, :], rsum[:, 0:1], None, ALU.mult)

            softmax.calls = 0
            dve.wait_ge(s_r_ps, 1)
            ch.link(nc.vector.tensor_tensor(rexp[:, :], psum[0:NB, 0, 0:NE], f1_br[:, :], ALU.add))
            softmax(rexp[:, :], rw[:, :]).then_inc(s_r, 1)
            dve.wait_ge(s_r, 1)
            dve.wait_ge(s_r_ps, 2)
            ch.link(nc.vector.reciprocal(scale[:, :], psum[0:NB, 1, 0:NE]))
            ch.link(nc.vector.tensor_scalar(scale[:, :], scale[:, :], CAPACITY / NN, 1.0, ALU.mult, ALU.min))
            ch.link(nc.vector.tensor_tensor(rw[:, :], rw[:, :], scale[:, :], ALU.mult))
            ch.link(softmax(rw[:, :], rw2[:, 0, :]))
            top2(ch, rw2[:, :, :], rw2b[:, :, :], [hot4[:, k:k + 1, :] for k in range(TOPK)],
                 rplace[:, :, :], rmax[:, :], NB, 1, rank8)
            ch.link(nc.vector.tensor_tensor(picked[:, :, :], hot4[:, :, :],
                                            rw2[:, 0:1, :].to_broadcast((NB, TOPK, NE)), ALU.mult))
            ch.link(nc.vector.tensor_reduce(topw[:, :], picked[:, :, :], AX_X, ALU.add))
            nc.vector.tensor_tensor(topd[:, :], topw[:, 1:2], topw[:, 0:1], ALU.subtract).then_inc(s_rin, 1)
            ch.link(nc.vector.tensor_tensor(picked[:, :, :], hot4[:, :, :],
                                            first_row[:, :].unsqueeze(1).to_broadcast((NB, TOPK, NE)), ALU.mult))
            ch.link(nc.vector.tensor_reduce(info[:, TOPK:2 * TOPK], picked[:, :, :], AX_X, ALU.add))
            nc.vector.tensor_tensor(hot_diag[:, :, :],
                                    hot4[:, :, :].rearrange("p k e -> p (k e)").unsqueeze(2)
                                    .to_broadcast((NB, TOPK * NE, NB)),
                                    ident[0:NB, 0:NB].unsqueeze(1).to_broadcast((NB, TOPK * NE, NB)), ALU.mult)\
                .then_inc(s_info, 1)
            dve.wait_ge(s_rexp, 3)
            ch.link(nc.vector.tensor_scalar(rsum[:, :], topd[:, :], 1.0, None, ALU.add))
            ch.link(nc.vector.reciprocal(info[:, 0:1], rsum[:, :]))
            ch.link(nc.vector.tensor_tensor(info[:, 1:2], topd[:, :], info[:, 0:1], ALU.mult))
            nc.vector.tensor_tensor(info_diag[:, :, :], info[:, :].unsqueeze(2).to_broadcast((NB, 2 * TOPK, NB)),
                                    ident[0:NB, 0:NB].unsqueeze(1).to_broadcast((NB, 2 * TOPK, NB)), ALU.mult)\
                .then_inc(s_info, 1)
            ch.link(nc.vector.tensor_scalar(wd2[:, :], hot4[:, 0, :], info[:, 0:1], None, ALU.mult))
            nc.vector.scalar_tensor_tensor(wdense[:, :], hot4[:, 1, :], info[:, 1:2], wd2[:, :],
                                           ALU.mult, ALU.add).then_inc(s_wd, 1)
            dve.wait_ge(s_sel_ps, 1)
            nc.vector.tensor_copy(places[:, :, :], psum[0:1, 2, TOPK * NB:2 * TOPK * NB]
                                  .rearrange("p (k b) -> p k b", k=TOPK)).then_inc(s_places, 1)
            nc.vector.tensor_copy(wtok[:, :, :], psum[:, 2, 0:TOPK * NB].rearrange("p (k b) -> p k b", k=TOPK))\
                .then_inc(s_wtok, 1)
            dve.wait_ge(s_sel_ps, 2)
            for k in range(TOPK):
                for c in range(FC):
                    ch.mark(nc.vector.tensor_tensor(
                        b1prod[:, FC * k + c, :, :],
                        psum[:, 3, k * NE * NB:(k + 1) * NE * NB].rearrange("p (e b) -> p b e", e=NE),
                        f1_b1[:, :, c].unsqueeze(1).to_broadcast((P, NB, NE)), ALU.mult))
            ch.settle()
            nc.vector.tensor_reduce(b1sel[:, :, :], b1prod[:, :, :, :], AX_X, ALU.add).then_inc(s_b1sel, 1)
            dve.wait_ge(s_sel_ps, 3)
            nc.vector.tensor_copy(wdT[:, :], psum[0:NE, 4, 0:NB]).then_inc(s_wdT, 1)
            dve.wait_ge(s_places, 1)
            dve.wait_ge(s_wtok, 1)

            def stage_w2(g, j):
                for k in range(TOPK):
                    place = dve.value_load(places[0:1, k, bass.ds(g * GB + j, 1)], min_val=0, max_val=(NE - 1) * HID)
                    ins = nc.vector.tensor_scalar(w2s[:, j, k, :], f1_w2[:, bass.ds(place, FC * D)],
                                                  wtok[:, k, bass.ds(g * GB + j, 1)], None, ALU.mult)
                ins.then_inc(s_w2s, 1)

            for j in range(GB):
                stage_w2(0, j)

            chF = Chain(dve, s_chF, LN4_LINKS)

            def body(g, first, last):
                chF.body(g)
                dve.wait_ge(s_xb, g + 1)
                if not first:
                    dve.wait_ge(s_yout, g)
                for j in range(GB):
                    n = GB * g + j
                    dve.wait_ge(s_o_ps, n + 1)
                    nc.vector.tensor_tensor(z[:, 2 * j:2 * j + 2, :].rearrange("p t d -> p (t d)"),
                                            psum[:, 4 + j % 2, 0:NN],
                                            xh3[:, bass.ds(g * GT + 2 * j, 2), :].rearrange("p t d -> p (t d)"),
                                            ALU.add).then_inc(s_z, 1)
                    if not last:
                        stage_w2(g + 1, j)
                dve.wait_ge(s_z, GB * g + GB)
                chained_layernorm(chF, lambda t: z[:, t, :])
                for t in range(GT):
                    chF.mark(nc.vector.scalar_tensor_tensor(z[:, t, :], z[:, t, :], mean[:, t:t + 1], gamma[:, :],
                                                            ALU.subtract, ALU.mult))
                if not first:
                    dve.wait_ge(s_out, 16 * g)
                chF.settle()
                for t in range(GT):
                    ins = nc.vector.scalar_tensor_tensor(yout[:, t, :], z[:, t, :], rstd[:, t:t + 1],
                                                         tile_of_x(g, t), ALU.mult, ALU.add)
                ins.then_inc(s_yout, 1)

            over_groups(dve, body)

        def ffn1_gpsimd(pool):
            phase3_done(pool)
            pool.wait_ge(s_places, 1)

            def stage_w1(g, j):
                for k in range(TOPK):
                    place = pool.value_load(places[0:1, k, bass.ds(g * GB + j, 1)], min_val=0, max_val=(NE - 1) * HID)
                    ins = nc.gpsimd.tensor_copy(w1s[:, j, k, :], f1_w1[:, bass.ds(place, HID)])
                ins.then_inc(s_w1s, 1)

            def weigh_b2(g, first):
                if first:
                    pool.wait_ge(s_wdT, 1)
                else:
                    pool.wait_ge(s_b2r_ps, g)
                nc.gpsimd.tensor_tensor(wb2[:, :, :],
                                        wdT[:, bass.ds(g * GB, GB)].unsqueeze(2).to_broadcast((NE, GB, D)),
                                        f1_b2[:, :].unsqueeze(1).to_broadcast((NE, GB, D)), ALU.mult)\
                    .then_inc(s_wb2, 1)

            def add_biases(g):
                pool.wait_ge(s_b2r, g + 1)
                xg = xres[:, bass.ds(g * GT, GT), :]
                nc.gpsimd.tensor_tensor(xg, xg, beta[:, :].unsqueeze(1).to_broadcast((P, GT, D)), ALU.add)
                for r in range(2):
                    xb = xh3[:, bass.ds(g * GT, GT), :].rearrange("p (b r) d -> p b r d", r=2)[:, :, r, :]
                    ins = nc.gpsimd.tensor_tensor(xb, xb, b2r[:, :, :], ALU.add)
                ins.then_inc(s_xb, 1)

            for j in range(GB):
                stage_w1(0, j)
            weigh_b2(0, True)

            def body(g, first, last):
                add_biases(g)
                if not last:
                    weigh_b2(g + 1, False)
                    for j in range(GB):
                        pool.wait_ge(s_h4_ps, TOPK * (GB * g + j + 1))
                        stage_w1(g + 1, j)

            over_groups(pool, body)

        block = ctx.enter_context(nc.Block())

        @block.sync
        def _(sp):
            gnn0_sync(sp)
            sp.wait_ge(s_adjT_out, 16 * NG)
            gnn1_sync(sp)
            ffn1_sync(sp)

        @block.gpsimd
        def _(pool):
            nc.gpsimd.memset(ident[:, :], 0.0).then_inc(s_poolc, 1)
            nc.gpsimd.memset(ones[:, :], 1.0).then_inc(s_const, 1)
            pool.wait_ge(s_poolc, 1)
            nc.gpsimd.affine_select(out=ident[:, :], in_=ident[:, :], compare_op=ALU.not_equal, fill=1.0,
                                    base=0, pattern=[[-1, P]], channel_multiplier=1).then_inc(s_const, 1)
            gnn0_gpsimd(pool)
            gnn1_gpsimd(pool)
            ffn1_gpsimd(pool)

        @block.tensor
        def _(pe):
            gnn0_tensor(pe)
            ffn0_tensor(pe)
            gnn1_tensor(pe)
            ffn1_tensor(pe)

        @block.scalar
        def _(act):
            gnn0_scalar(act)
            ffn0_scalar(act)
            gnn1_scalar(act)
            ffn1_scalar(act)

        @block.vector
        def _(dve):
            nc.vector.memset(kheadT[:, :, :], 0.0).then_inc(s_const, 1)
            for e in range(NE):
                nc.vector.memset(rank8[:, e:e + 1], float(NE - e))
            gnn0_vector(dve)
            ffn0_vector(dve)
            gnn1_vector(dve)
            ffn1_vector(dve)


_INS = ["x", "adj", "L0_gnn_W_lin", "L0_gnn_b_lin", "L0_gnn_W_q", "L0_gnn_W_k", "L0_gnn_ln_g", "L0_gnn_ln_b",
        "L0_ffn_Wg", "L0_ffn_bg", "L0_ffn_W1", "L0_ffn_b1", "L0_ffn_W2", "L0_ffn_b2",
        "L1_gnn_W_w", "L1_gnn_W_b", "L1_gnn_a_w", "L1_gnn_a_b",
        "L1_ffn_Wr", "L1_ffn_br", "L1_ffn_W1", "L1_ffn_b1", "L1_ffn_W2", "L1_ffn_b2",
        "L1_ffn_gamma", "L1_ffn_beta"]
_OUTS = [((NB, NN, D), "float32")]


def kernel(**inputs):
    import numpy as _np
    import concourse.bacc as _bacc
    from concourse import mybir as _mybir
    from concourse.bass_utils import run_bass_kernel_spmd as _run

    nc = _bacc.Bacc("TRN2", target_bir_lowering=False, num_devices=1)
    arrays, tensors = {}, {}
    for name in _INS:
        a = _np.ascontiguousarray(inputs[name])
        arrays[f"in_{name}_dram"] = a
        tensors[name] = nc.dram_tensor(f"in_{name}_dram", a.shape, _mybir.dt.from_np(a.dtype),
                                       kind="ExternalInput").ap()
    outs = [nc.dram_tensor(f"out_{i}_dram", shape, _mybir.dt.from_np(_np.dtype(dtype)), kind="ExternalOutput").ap()
            for i, (shape, dtype) in enumerate(_OUTS)]
    build_program(nc, tensors, outs[0])
    r = _run(nc, [arrays], core_ids=[0])
    got = tuple(r.results[0][f"out_{i}_dram"] for i in range(len(_OUTS)))
    return got[0]
```

```python
from contextlib import ExitStack

import concourse.bass as bass
from concourse import mybir

F32 = mybir.dt.float32
I32 = mybir.dt.int32
ALU = mybir.AluOpType
ACT = mybir.ActivationFunctionType
AX_X = mybir.AxisListType.X

P = 128
D = 128
NB = 32
NN = 256
HEADS = 4
HD = D // HEADS
GB = 4
NG = NB // GB
GT = GB * NN // P
NT = NB * NN // P
GTOK = GB * NN
NE = 8
HID = 256
FC = HID // P
TOPK = 2
EPS = 1e-5
BANK = 512
SLOTS = 2 * P
STRIDE = NT * P + SLOTS
NBLK = TOPK * NT * P // SLOTS + NE
SPARE = NE
ROW = D + 2
JUNK = TOPK * NT * P
PADS = NE * SLOTS // P
UNROLL = 4
DEG_MIN = 2.0 ** -64
RSQRT_MAGIC = float(0x5F3759DF)


class Chain:

    def __init__(self, engine, sem, per):
        self.engine, self.sem, self.per, self.base, self.k = engine, sem, per, 0, 0

    def body(self, n):
        assert self.k in (0, self.per), (self.k, self.per)
        self.base, self.k = n * self.per, 0

    def mark(self, ins):
        self.k += 1
        ins.then_inc(self.sem, 1)

    def settle(self):
        self.engine.wait_ge(self.sem, self.base + self.k)

    def link(self, ins):
        self.mark(ins)
        self.settle()


def build_program(nc, I, out):
    with ExitStack() as ctx:
        def sb(name, shape, dt=F32):
            return ctx.enter_context(nc.sbuf_tensor(name, shape, dt))

        def sem(name):
            return ctx.enter_context(nc.semaphore(name))

        x_dram = I["x"].rearrange("(g b) (t p) d -> g p (b t) d", b=GB, p=P)
        adj_dram = I["adj"].rearrange("(g b) (c p) y -> g p (b c) y", b=GB, p=P)
        out_dram = out.rearrange("(g b) (t p) d -> g p (b t) d", b=GB, p=P)
        adjT_dram = nc.dram_tensor("adjT_scratch", (NG, P, GB * 2 * NN), F32).ap()

        ident = sb("ident", [P, P])
        ones = sb("ones", [P, P])
        xres = sb("xres", [P, NT, D])

        f0_wg = sb("f0_wg", [P, NE])
        f0_bg = sb("f0_bg", [P, NE])
        f0_w = sb("f0_w", [P, NE, 2 * HID])
        f0_b1 = sb("f0_b1", [P, NE * FC])
        f0_b2 = sb("f0_b2", [P, NE * D])
        s_w2 = sem("s_w2")
        rank8 = sb("rank8", [P, NE])

        before = sb("before", [P, P])
        token_no = sb("token_no", [P, NT])
        region = sb("region", [P, NE])
        block_no = sb("block_no", [P, NBLK])
        block_lo = sb("block_lo", [P, NT * P // SLOTS])
        pad_no = sb("pad_no", [P, NE, SLOTS // P])
        pad_rows = sb("pad_rows", [P, PADS, ROW])
        s_const2 = sem("s_const2")
        CONST2 = 8
        rows_dram = nc.dram_tensor("expert_rows", (NE * STRIDE + SPARE * SLOTS, ROW), F32).ap()
        y_dram = nc.dram_tensor("expert_outputs", (JUNK + 2 * PADS * P, D), F32).ap()

        stats = sb("stats", [P, GT, 6])
        msum = sb("msum", [P, GT])
        mdiff = sb("mdiff", [P, GT])
        sqsum = sb("sqsum", [P, GT])
        mean = sb("mean", [P, GT])
        veps = sb("veps", [P, GT])
        rstd = sb("rstd", [P, GT])
        newt = sb("newt", [P, GT])

        psum = ctx.enter_context(nc.psum_tensor("psum", [P, 8, BANK], F32))

        s_const = sem("s_const")
        pool_token = sb("pool_token", [P, 1])
        act_token = sb("act_token", [P, 1])
        s_out = sem("s_out")

        def chained_layernorm(ch, src_of):
            for t in range(GT):
                ch.mark(nc.vector.bn_stats(stats[:, t, :], src_of(t)))
            ch.settle()
            mean_a, sq_a, mean_b, sq_b = (stats[:, :, i] for i in (1, 2, 4, 5))
            ch.mark(nc.vector.tensor_tensor(msum[:, :], mean_a, mean_b, ALU.add))
            ch.mark(nc.vector.tensor_tensor(mdiff[:, :], mean_a, mean_b, ALU.subtract))
            ch.mark(nc.vector.tensor_tensor(sqsum[:, :], sq_a, sq_b, ALU.add))
            ch.settle()
            ch.mark(nc.vector.tensor_scalar(mean[:, :], msum[:, :], 0.5, None, ALU.mult))
            ch.mark(nc.vector.scalar_tensor_tensor(mdiff[:, :], mdiff[:, :], 0.25, mdiff[:, :],
                                                   ALU.mult, ALU.mult))
            ch.mark(nc.vector.tensor_scalar(sqsum[:, :], sqsum[:, :], 1.0 / D, EPS, ALU.mult, ALU.add))
            ch.settle()
            ch.link(nc.vector.tensor_tensor(veps[:, :], sqsum[:, :], mdiff[:, :], ALU.add))
            ch.link(nc.vector.tensor_scalar(rstd[:, :].bitcast(I32), veps[:, :].bitcast(I32),
                                            -0.5, RSQRT_MAGIC, ALU.mult, ALU.add))
            for _ in range(3):
                ch.link(nc.vector.scalar_tensor_tensor(newt[:, :], rstd[:, :], -0.5, rstd[:, :],
                                                       ALU.mult, ALU.mult))
                ch.link(nc.vector.tensor_tensor(newt[:, :], newt[:, :], veps[:, :], ALU.mult))
                ch.link(nc.vector.scalar_tensor_tensor(rstd[:, :], newt[:, :], 1.5, rstd[:, :],
                                                       ALU.add, ALU.mult))

        LN_LINKS = GT + 6 + 2 + 9

        def tile_of_x(g, t):
            return xres[:, bass.ds(g * GT + t, 1), :].rearrange("p a d -> p (a d)")

        ph1 = ExitStack()
        ctx.push(ph1)

        def sb1(name, shape, dt=F32):
            return ph1.enter_context(nc.sbuf_tensor(name, shape, dt))

        w_k, w_q, w_lin = sb1("w_k", [P, D]), sb1("w_q", [P, D]), sb1("w_lin", [P, D])
        b_lin = sb1("b_lin", [P, 1])
        ln_g, ln_b = sb1("ln_g", [P, D]), sb1("ln_b", [P, D])
        adj_in = sb1("adj_in", [P, GT, NN])
        adjT = sb1("adjT", [P, GB, 2, NN])
        xh = sb1("xh", [P, GT, D])
        xhT = sb1("xhT", [P, GTOK])
        raw = sb1("raw", [P, 3, GTOK])
        kqxT = sb1("kqxT", [P, 3, GTOK])
        kheadT = sb1("kheadT", [P, HEADS, GTOK])
        att = sb1("att", [P, 2, 2, 2, NN])
        adj_h = sb1("adj_h", [P, GB, 2, 2, 2, NN])
        deg = sb1("deg", [P, GTOK])
        dis = sb1("dis", [P, GTOK])
        xs = sb1("xs", [P, GT, D])
        xsT = sb1("xsT", [P, GTOK])
        yT = sb1("yT", [P, NN])
        y_sb = sb1("y_sb", [P, GT, D])
        y_n = sb1("y_n", [P, GT, D])

        s_w1 = sem("s_w1")
        s_x = sem("s_x")
        s_adj = sem("s_adj")
        s_khead = sem("s_khead")
        s_adjT_out = sem("s_adjT_out")
        s_xhT_ps, s_adjT_ps, s_proj_ps = sem("s_xhT_ps"), sem("s_adjT_ps"), sem("s_proj_ps")
        s_score_ps, s_deg_ps = sem("s_score_ps"), sem("s_deg_ps")
        s_xs_ps, s_yT_ps, s_y_ps = sem("s_xs_ps"), sem("s_yT_ps"), sem("s_y_ps")
        s_xhT, s_adjT, s_raw, s_att = sem("s_xhT"), sem("s_adjT"), sem("s_raw"), sem("s_att")
        s_ln, s_dis, s_xs, s_y = sem("s_ln"), sem("s_dis"), sem("s_xs"), sem("s_y")
        s_xh, s_kqx, s_adjh, s_deg = sem("s_xh"), sem("s_kqx"), sem("s_adjh"), sem("s_deg")
        s_degpos, s_xsT, s_yT, s_yn = sem("s_degpos"), sem("s_xsT"), sem("s_yT"), sem("s_yn")
        s_chA, s_chB = sem("s_chA"), sem("s_chB")
        s_x1 = sem("s_x1")
        s_poolc = sem("s_poolc")

        two01 = psum[:, 0:2, :].rearrange("p a n -> p (a n)")
        two23 = psum[:, 2:4, :].rearrange("p a n -> p (a n)")
        deg_ps, xs_ps, yT_ps, y_ps = (psum[:, 4 + i, :] for i in range(4))

        def for_groups(engine, body):
            body(0, True, False)
            with engine.Fori(1, NG) as g:
                body(g, True, True)
            body(NG, False, True)

        def gnn0_sync(sp):
            for dst, name in ((w_k, "L0_gnn_W_k"), (w_q, "L0_gnn_W_q"), (w_lin, "L0_gnn_W_lin")):
                sp.dma_start(dst[:, :], I[name]).then_inc(s_w1, 16)
            sp.dma_start(b_lin[:, :], I["L0_gnn_b_lin"].rearrange("(p a) -> p a", a=1)).then_inc(s_w1, 16)
            for dst, name in ((ln_g, "L0_gnn_ln_g"), (ln_b, "L0_gnn_ln_b")):
                sp.dma_start(dst[:, :], I[name].rearrange("(a n) -> a n", a=1).to_broadcast((P, D)))\
                    .then_inc(s_w1, 16)
            sp.dma_start(xres[:, 0:GT, :], x_dram[0]).then_inc(s_x, 16)
            sp.dma_start(adj_in[:, :, :], adj_dram[0]).then_inc(s_adj, 16)
            load_weights(sp)

            def split_heads(g):
                sp.wait_ge(s_kqx, 3 * g + 1)
                for h in range(HEADS):
                    rows = slice(HD * h, HD * (h + 1))
                    sp.dma_start(kheadT[rows, h, :], kqxT[rows, 0, :]).then_inc(s_khead, 16)

            sp.wait_ge(s_const, 3)
            split_heads(0)
            with sp.Fori(1, NG) as g:
                sp.wait_ge(s_x, 16 * g)
                sp.dma_start(xres[:, bass.ds(g * GT, GT), :], x_dram[g]).then_inc(s_x, 16)
                sp.wait_ge(s_adjT_ps, GB * g)
                sp.wait_ge(s_adj, 16 * g)
                sp.dma_start(adj_in[:, :, :], adj_dram[g]).then_inc(s_adj, 16)
                sp.wait_ge(s_khead, 64 * g)
                sp.wait_ge(s_score_ps, 8 * g)
                split_heads(g)

        def gnn0_tensor(pe):
            pe.wait_ge(s_const, 3)
            pe.wait_ge(s_w1, 6 * 16)

            def body(g, a, b):
                if a:
                    pe.wait_ge(s_xh, g + 1)
                    if b:
                        pe.wait_ge(s_att, 8 * g)
                    for t in range(GT):
                        ins = nc.tensor.transpose(two01[:, t * P:(t + 1) * P], xh[:, t, :], ident[:, :])
                    ins.then_inc(s_xhT_ps, 1)

                    def transpose_adj(j):
                        if j == 0:
                            pe.wait_ge(s_adj, 16 * (g + 1))
                            if b:
                                pe.wait_ge(s_deg, GB * g)
                        bank = psum[:, 4 + j, :]
                        for c in range(2):
                            for r in range(2):
                                ins = nc.tensor.transpose(
                                    bank[:, c * NN + r * P:c * NN + (r + 1) * P],
                                    adj_in[:, 2 * j + r, c * P:(c + 1) * P], ident[:, :])
                        ins.then_inc(s_adjT_ps, 1)

                    def project(n, w, dst):
                        for c in range(2):
                            ins = nc.tensor.matmul(dst[:, c * BANK:(c + 1) * BANK], w[:, :],
                                                   xhT[:, c * BANK:(c + 1) * BANK], start=True, stop=True)
                        ins.then_inc(s_proj_ps, 1)

                    transpose_adj(0)
                    transpose_adj(1)
                    pe.wait_ge(s_xhT, g + 1)
                    project(0, w_k, two23)
                    project(1, w_q, two01)
                    transpose_adj(2)
                    transpose_adj(3)
                    pe.wait_ge(s_raw, 3 * g + 1)
                    project(2, w_lin, two23)

                def degrees(j):
                    pe.wait_ge(s_adjh, 8 * g + 2 * j + 2)
                    if j == 0:
                        pe.wait_ge(s_adjT, GB * g + 1)
                    else:
                        pe.wait_ge(s_deg, GB * g + j)
                    for c in range(2):
                        for h in range(HEADS):
                            ins = nc.tensor.matmul(deg_ps[HD * h:HD * (h + 1), 0:NN], ones[:, 0:HD],
                                                   adj_h[:, j, h // 2, h % 2, c, :], start=(c == 0), stop=(c == 1))
                    ins.then_inc(s_deg_ps, 1)

                def scores(j, u):
                    if j == 0 and u == 0:
                        pe.wait_ge(s_khead, 64 * g + 64)
                        pe.wait_ge(s_kqx, 3 * g + 2)
                    if j == 0:
                        pe.wait_ge(s_raw, 3 * g + 2 + u)
                    else:
                        pe.wait_ge(s_att, 8 * g + 2 * j - 1 + u)
                    for c in range(2):
                        for h in (2 * u, 2 * u + 1):
                            ins = nc.tensor.matmul(
                                psum[:, h, c * NN:(c + 1) * NN],
                                kheadT[:, h, j * NN + c * P:j * NN + (c + 1) * P],
                                kqxT[:, 1, j * NN:(j + 1) * NN], start=True, stop=True)
                    ins.then_inc(s_score_ps, 1)

                for j in range(GB):
                    n = GB * (g - 1) + j
                    if a:
                        scores(j, 0)
                    if b:
                        if j == 0:
                            pe.wait_ge(s_xsT, g)
                            if a:
                                pe.wait_ge(s_adjT, GB * g + 4)
                        else:
                            pe.wait_ge(s_xs, n)
                        for t in range(2):
                            ins = nc.tensor.transpose(xs_ps[:, t * P:(t + 1) * P],
                                                      xsT[:, j * NN + t * P:j * NN + (t + 1) * P], ident[:, :])
                        ins.then_inc(s_xs_ps, 1)
                    if a:
                        scores(j, 1)
                    if b:
                        pe.wait_ge(s_xs, n + 1)
                        if j > 0:
                            pe.wait_ge(s_yT, n)
                        for c in range(2):
                            for h in range(HEADS):
                                ins = nc.tensor.matmul(yT_ps[HD * h:HD * (h + 1), 0:NN],
                                                       xs[:, 2 * j + c, HD * h:HD * (h + 1)],
                                                       adj_h[:, j, h // 2, h % 2, c, :], start=(c == 0), stop=(c == 1))
                        ins.then_inc(s_yT_ps, 1)
                    if a and j > 0:
                        degrees(j - 1)
                    if b:
                        pe.wait_ge(s_yT, n + 1)
                        if j > 0:
                            pe.wait_ge(s_y, n)
                        for t in range(2):
                            ins = nc.tensor.transpose(y_ps[:, t * P:(t + 1) * P],
                                                      yT[:, t * P:(t + 1) * P], ident[:, :])
                        ins.then_inc(s_y_ps, 1)
                if a:
                    degrees(GB - 1)
                if b:
                    pe.wait_ge(s_y, GB * g)

            for_groups(pe, body)

        def gnn0_scalar(act):
            act.wait_ge(s_w1, 6 * 16)
            act.wait_ge(s_const, 3)

            def body(g, a, b):
                def copy_adj(j):
                    act.wait_ge(s_adjT_ps, GB * g + j + 1)
                    nc.scalar.activation(adjT[:, j, :, :].rearrange("p c n -> p (c n)"),
                                         psum[:, 4 + j, :], ACT.Copy).then_inc(s_adjT, 1)

                def copy_projection(n, src):
                    act.wait_ge(s_proj_ps, 3 * g + n + 1)
                    if n < 2:
                        nc.scalar.activation(raw[:, n, :], src, ACT.Copy).then_inc(s_raw, 1)
                    else:
                        nc.scalar.activation(raw[:, n, :], src, ACT.Identity, bias=b_lin[:, :])\
                            .then_inc(s_raw, 1)

                if a:
                    act.wait_ge(s_xhT_ps, g + 1)
                    nc.scalar.activation(xhT[:, :], two01, ACT.Copy).then_inc(s_xhT, 1)
                    if b:
                        act.wait_ge(s_kqx, 3 * g)
                    copy_projection(0, two23)
                    copy_projection(1, two01)
                if b:
                    act.wait_ge(s_degpos, g)
                    nc.scalar.activation(dis[:, :], dis[:, :], ACT.Ln).then_inc(s_ln, 1)
                    act.wait_ge(s_ln, g)
                    nc.scalar.activation(dis[:, :], dis[:, :], ACT.Exp, scale=-0.5).then_inc(s_dis, 1)
                if a:
                    copy_projection(2, two23)
                    if b:
                        act.wait_ge(s_adjh, 8 * g)
                        act.wait_ge(s_adjT_out, 16 * g)
                    for j in range(GB):
                        copy_adj(j)
                    act.wait_ge(s_adjT, GB * g + GB)
                    act.dma_start(adjT_dram[g], adjT[:, :, :, :].rearrange("p b c n -> p (b c n)"))\
                        .then_inc(s_adjT_out, 16)

                def copy_y(j):
                    n = GB * (g - 1) + j
                    act.wait_ge(s_y_ps, n + 1)
                    nc.scalar.activation(y_sb[:, 2 * j:2 * j + 2, :].rearrange("p t d -> p (t d)"),
                                         y_ps[:, 0:NN], ACT.Copy).then_inc(s_y, 1)

                def sigmoid(j, u):
                    act.wait_ge(s_score_ps, 8 * g + 2 * j + u + 1)
                    if b or j > 0:
                        act.wait_ge(s_adjh, 8 * g + 2 * j - 1 + u)
                    nc.scalar.activation(att[:, u, :, :, :].rearrange("p h c n -> p (h c n)"),
                                         (two01, two23)[u], ACT.Sigmoid, scale=float(HD) ** -0.5)\
                        .then_inc(s_att, 1)

                for j in range(GB):
                    if a:
                        sigmoid(j, 0)
                    if b:
                        act.wait_ge(s_xs_ps, GB * (g - 1) + j + 1)
                        nc.scalar.activation(xs[:, 2 * j:2 * j + 2, :].rearrange("p t d -> p (t d)"),
                                             xs_ps[:, 0:NN], ACT.Copy).then_inc(s_xs, 1)
                        if j > 0:
                            copy_y(j - 1)
                    if a:
                        sigmoid(j, 1)
                if b:
                    copy_y(GB - 1)

            for_groups(act, body)

        LN0_LINKS = LN_LINKS
        CHB = 1 + LN_LINKS

        def gnn0_vector(dve):
            chA = Chain(dve, s_chA, LN0_LINKS)
            chB = Chain(dve, s_chB, CHB)

            def stats_in(g):
                chA.body(g)
                dve.wait_ge(s_x, 16 * (g + 1))
                chained_layernorm(chA, lambda t: tile_of_x(g, t))

            def normalise_in(g):
                for t in range(GT):
                    ins = nc.vector.tensor_scalar(xh[:, t, :], tile_of_x(g, t), mean[:, t:t + 1],
                                                  rstd[:, t:t + 1], ALU.subtract, ALU.mult)
                ins.then_inc(s_xh, 1)

            def leaky(g, n):
                dve.wait_ge(s_raw, 3 * g + n + 1)
                nc.vector.scalar_tensor_tensor(kqxT[:, n, :], raw[:, n, :], 0.01, raw[:, n, :],
                                               ALU.mult, ALU.max).then_inc(s_kqx, 1)

            def body(g, a, b, more=True):
                if b:
                    chB.body(g - 1)
                    dve.wait_ge(s_dis, g)
                    chB.link(nc.vector.scalar_tensor_tensor(dis[:, :], deg[:, :], 0.0, dis[:, :],
                                                            ALU.is_gt, ALU.mult))
                    nc.vector.tensor_tensor(xsT[:, :], kqxT[:, 2, :], dis[:, :], ALU.mult).then_inc(s_xsT, 1)
                    if a:
                        dve.wait_ge(s_xsT, g)
                if a:
                    leaky(g, 2)
                if a and more:
                    stats_in(g + 1)
                    dve.wait_ge(s_xhT_ps, g + 1)
                    normalise_in(g + 1)

                def weigh(j, c):
                    dve.wait_ge(s_att, 8 * g + 2 * j + c + 1)
                    if j == 0 and c == 0:
                        dve.wait_ge(s_adjT, GB * g + GB)
                    if b and c == 0:
                        dve.wait_ge(s_yT_ps, GB * (g - 1) + j + 1)
                    nc.vector.tensor_tensor(
                        adj_h[:, j, c, :, :, :].rearrange("p h c n -> p h (c n)"),
                        att[:, c, :, :, :].rearrange("p h c n -> p h (c n)"),
                        adjT[:, j, :, :].rearrange("p c n -> p (c n)").unsqueeze(1).to_broadcast((P, 2, 2 * NN)),
                        ALU.mult).then_inc(s_adjh, 1)

                def degrees(j):
                    dve.wait_ge(s_deg_ps, GB * g + j + 1)
                    if j == 0 and b:
                        dve.wait_ge(s_xsT, g)
                    nc.vector.tensor_copy(deg[:, j * NN:(j + 1) * NN], deg_ps[:, 0:NN]).then_inc(s_deg, 1)

                for j in range(GB):
                    if b:
                        n = GB * (g - 1) + j
                        dve.wait_ge(s_yT_ps, n + 1)
                        if j > 0:
                            dve.wait_ge(s_y_ps, n)
                        nc.vector.tensor_tensor(yT[:, :], yT_ps[:, 0:NN], dis[:, j * NN:(j + 1) * NN],
                                                ALU.mult).then_inc(s_yT, 1)
                    if a:
                        weigh(j, 0)
                        weigh(j, 1)
                        if j > 0:
                            degrees(j - 1)
                if a:
                    degrees(GB - 1)
                    if b:
                        dve.wait_ge(s_yT, GB * g)
                    dve.wait_ge(s_deg, GB * g + GB)
                    nc.vector.tensor_scalar(dis[:, :], deg[:, :], DEG_MIN, None, ALU.max).then_inc(s_degpos, 1)
                if b:
                    dve.wait_ge(s_y, GB * g)
                    chained_layernorm(chB, lambda t: y_sb[:, t, :])
                if a and more:
                    dve.wait_ge(s_khead, 64 * g + 64)
                    leaky(g + 1, 0)
                    leaky(g + 1, 1)
                if b:
                    dve.wait_ge(s_x1, g)
                    for t in range(GT):
                        ins = nc.vector.tensor_scalar(y_n[:, t, :], y_sb[:, t, :], mean[:, t:t + 1],
                                                      rstd[:, t:t + 1], ALU.subtract, ALU.mult)
                    ins.then_inc(s_yn, 1)

            stats_in(0)
            normalise_in(0)
            leaky(0, 0)
            leaky(0, 1)
            body(0, True, False)
            with dve.Fori(1, NG - 1) as g:
                body(g, True, True)
            body(NG - 1, True, True, more=False)
            body(NG, False, True)

        def gnn0_gpsimd(pool):
            nc.gpsimd.memset(y_n[:, :, :], 0.0).then_inc(s_x1, 1)
            pool.wait_ge(s_w1, 6 * 16)
            with pool.Fori(1, NG + 1) as g:
                pool.wait_ge(s_yn, g)
                nc.gpsimd.tensor_tensor(y_n[:, :, :], y_n[:, :, :],
                                        ln_g[:, :].unsqueeze(1).to_broadcast((P, GT, D)), ALU.mult)\
                    .then_inc(s_poolc, 1)
                pool.wait_ge(s_poolc, 2 * g)
                nc.gpsimd.tensor_tensor(y_n[:, :, :], y_n[:, :, :],
                                        ln_b[:, :].unsqueeze(1).to_broadcast((P, GT, D)), ALU.add)\
                    .then_inc(s_poolc, 1)
                pool.wait_ge(s_poolc, 2 * g + 1)
                xg = xres[:, bass.ds((g - 1) * GT, GT), :]
                nc.gpsimd.tensor_tensor(xg, y_n[:, :, :], xg, ALU.add).then_inc(s_x1, 1)

        s_ph1 = s_x1
        ph1.close()

        def load_weights(sp):
            sp.dma_start(f0_wg[:, :], I["L0_ffn_Wg"]).then_inc(s_w2, 16)
            sp.dma_start(f0_bg[:, :], I["L0_ffn_bg"].rearrange("(a n) -> a n", a=1).to_broadcast((P, NE)))\
                .then_inc(s_w2, 16)
            sp.dma_start(f0_w[:, :, 0:HID], I["L0_ffn_W1"].rearrange("e d h -> d e h")).then_inc(s_w2, 16)
            for c in range(FC):
                lo = HID + c * D
                sp.dma_start(f0_w[:, :, lo:lo + D], I["L0_ffn_W2"][:, c * P:(c + 1) * P, :].rearrange("e p d -> p e d"))\
                    .then_inc(s_w2, 16)
            with nc.allow_non_contiguous_dma(reason="2048 biases, one per partition"):
                for e in range(NE):
                    sp.dma_start(f0_b1[:, e * FC:(e + 1) * FC], I["L0_ffn_b1"][e].rearrange("(c p) -> p c", p=P))\
                        .then_inc(s_w2, 16)
            sp.dma_start(f0_b2[:, :], I["L0_ffn_b2"].rearrange("(a e) d -> a (e d)", a=1).to_broadcast((P, NE * D)))\
                .then_inc(s_w2, 16)
            sp.wait_ge(s_const2, CONST2)
            sp.dma_start(rows_dram[NE * STRIDE:NE * STRIDE + PADS * P, :].rearrange("(q p) d -> p q d", p=P),
                         pad_rows[:, :, :]).then_inc(s_w2, 16)

        W2_LOADS = 16 * (4 + FC + NE + 1)

        def phase1_done(engine):
            engine.wait_ge(s_ph1, NG + 1)
            engine.wait_ge(s_adjT_out, 16 * NG)

        ph2 = ExitStack()
        ctx.push(ph2)

        def sb2(name, shape, dt=F32):
            return ph2.enter_context(nc.sbuf_tensor(name, shape, dt))

        rows = sb2("rows", [P, 2, GT, ROW])
        xh1T = sb2("xh1T", [P, GTOK])
        gate = sb2("gate", [P, GT, NE])
        gate2 = sb2("gate2", [P, GT, NE])
        hot = sb2("hot", [P, TOPK, GT, NE])
        place = sb2("place", [P, GT, NE])
        gmax = sb2("gmax", [P, GT])
        emask = sb2("emask", [P, GT + 1, NE])
        pos = sb2("pos", [P, GT, NE])
        posk = sb2("posk", [P, TOPK, GT, NE])
        row_of = sb2("row_of", [P, 2, TOPK, GT], I32)
        filled = sb2("filled", [P, NE])
        total = sb2("total", [P, NE])
        full = sb2("full", [P, NE, NT * P // SLOTS])
        steps_of = sb2("steps_of", [P, NE])
        end_a, end_b = sb2("end_a", [P, NE]), sb2("end_b", [P, NE])
        pad_at = sb2("pad_at", [P, NE, SLOTS // P], I32)
        past = sb2("past", [P, NBLK, NE])
        skip = sb2("skip", [P, NE])
        passed = sb2("passed", [1, NBLK, NE])
        expert = sb2("expert", [P, NBLK])
        expert_rank = sb2("expert_rank", [P, NBLK])
        expert_i = sb2("expert_i", [1, NBLK], I32)
        row_f = sb2("row_f", [1, NBLK])
        row_i = sb2("row_i", [1, NBLK], I32)
        xin = sb2("xin", [P, UNROLL, SLOTS // P, ROW])
        xinT = sb2("xinT", [P, UNROLL, SLOTS])
        wst = sb2("wst", [P, UNROLL, 2 * HID])
        hT = sb2("hT", [P, UNROLL, FC, SLOTS])
        y_rows = sb2("y_rows", [P, UNROLL, SLOTS // P, D])
        higher = sb2("higher", [P, UNROLL, SLOTS // P])
        y_at = sb2("y_at", [P, UNROLL, SLOTS // P], I32)

        s_xh1, s_xh1T_ps, s_xh1T = sem("s_xh1"), sem("s_xh1T_ps"), sem("s_xh1T")
        s_gate_ps, s_mask, s_rank_ps, s_rows = sem("s_gate_ps"), sem("s_mask"), sem("s_rank_ps"), sem("s_rows")
        s_sent = [sem(f"s_sent{u}") for u in range(2)]
        s_chC, s_chT = sem("s_chC"), sem("s_chT")
        s_pads, s_padded, s_table = sem("s_pads"), sem("s_padded"), sem("s_table")
        s_xin = [sem(f"s_xin{u}") for u in range(UNROLL)]
        s_y_sent = [sem(f"s_y_sent{u}") for u in range(UNROLL)]
        s_bT_ps, s_bT, s_wst, s_bh_ps, s_bh, s_bo_ps, s_y_rows, s_higher, s_y_at = (
            sem("s_bT_ps"), sem("s_bT"), sem("s_wst"), sem("s_bh_ps"), sem("s_bh"), sem("s_bo_ps"),
            sem("s_y_rows"), sem("s_higher"), sem("s_y_at"))
        s_x2 = sem("s_x2")
        s_pool_step = sem("s_pool_step")

        def top2(ch, sc, sc2, oh, pl, mx, rows, tiles, reverse):
            rev = reverse[0:rows, :].unsqueeze(1).to_broadcast((rows, tiles, NE))

            def wide(v):
                return v.unsqueeze(2).to_broadcast((rows, tiles, NE))

            for k in range(TOPK):
                src = (sc, sc2)[k]
                ch.link(nc.vector.tensor_reduce(mx, src, AX_X, ALU.max))
                ch.link(nc.vector.tensor_tensor(pl, src, wide(mx), ALU.is_equal))
                ch.link(nc.vector.tensor_tensor(pl, pl, rev, ALU.mult))
                ch.link(nc.vector.tensor_reduce(mx, pl, AX_X, ALU.max))
                ch.link(nc.vector.tensor_tensor(oh[k], pl, wide(mx), ALU.is_equal))
                if k == 0:
                    ch.link(nc.vector.scalar_tensor_tensor(sc2, oh[0], -3.0e38, sc, ALU.mult, ALU.add))

        TOP2_LINKS = 11

        def over_pairs(engine, body):
            body(0, True)
            with engine.Fori(1, NG // 2) as i:
                body(i, False)

        def over_steps(engine, body):
            body(0, True, False)
            with engine.Fori(1, NBLK // UNROLL - 1) as i:
                body(i, False, False)
            body(NBLK // UNROLL - 1, False, True)

        def all_sent(engine):
            for u in range(2):
                engine.wait_ge(s_sent[u], 16 * TOPK * GT * NG // 2)
            engine.wait_ge(s_padded, 16 * NE * SLOTS // P)

        def ffn0_sync(sp):
            all_sent(sp)
            sp.wait_ge(s_w2, W2_LOADS)
            sp.wait_ge(s_table, 3)

            def body(i, first, last):
                for u in range(UNROLL):
                    n = UNROLL * i + u
                    at = sp.value_load(row_i[0:1, bass.ds(n, 1)], min_val=0, max_val=NE * STRIDE + (SPARE - 1) * SLOTS)
                    if not first:
                        sp.wait_ge(s_higher, n - UNROLL + 1)
                        sp.wait_ge(s_bT_ps, n - UNROLL + 1)
                        sp.wait_ge(s_y_at, n - UNROLL + 1)
                    sp.dma_start(xin[:, u, :, :], rows_dram[bass.ds(at, SLOTS), :].rearrange("(t p) d -> p t d", p=P))\
                        .then_inc(s_xin[u], 16)

            over_steps(sp, body)

        def ffn0_tensor(pe):
            phase1_done(pe)
            pe.wait_ge(s_w2, W2_LOADS)
            pe.wait_ge(s_const2, CONST2)

            def route(i, first):
                for u in range(2):
                    g = 2 * i + u
                    pe.wait_ge(s_xh1, g + 1)
                    for t in range(GT):
                        ins = nc.tensor.transpose(two01[:, t * P:(t + 1) * P], rows[:, u, t, 0:D], ident[:, :])
                    ins.then_inc(s_xh1T_ps, 1)
                    pe.wait_ge(s_xh1T, g + 1)
                    for t in range(GT):
                        ins = nc.tensor.matmul(psum[:, 6, t * NE:(t + 1) * NE], xh1T[:, t * P:(t + 1) * P],
                                               f0_wg[:, :], start=True, stop=True)
                    ins.then_inc(s_gate_ps, 1)
                    pe.wait_ge(s_mask, g + 1)
                    flat = emask[:, :, :].rearrange("p t e -> p (t e)")
                    wide = (GT + 1) * NE
                    nc.tensor.matmul(psum[:, 7, 0:wide], before[:, :], flat, start=True, stop=False)
                    for t in range(1, GT + 1):
                        ins = nc.tensor.matmul(psum[:, 7, t * NE:wide], ones[:, :], flat[:, 0:wide - t * NE],
                                               start=False, stop=(t == GT))
                    ins.then_inc(s_rank_ps, 1)

            over_pairs(pe, route)

            def transpose_in(i, u):
                n = UNROLL * i + u
                pe.wait_ge(s_xin[u], 16 * i + 16)
                if not (isinstance(i, int) and i == 0 and u < 2):
                    pe.wait_ge(s_bT, n - 1)
                for r in range(SLOTS // P):
                    ins = nc.tensor.transpose(psum[:, u % 2, r * P:(r + 1) * P], xin[:, u, r, 0:D], ident[:, :])
                ins.then_inc(s_bT_ps, 1)

            def hidden(i, u, first):
                n = UNROLL * i + u
                pe.wait_ge(s_bT, n + 1)
                pe.wait_ge(s_wst, n + 1)
                if not first:
                    pe.wait_ge(s_bh, n - UNROLL + 1)
                for c in range(FC):
                    ins = nc.tensor.matmul(psum[:, 2 + u, c * SLOTS:(c + 1) * SLOTS], wst[:, u, c * P:(c + 1) * P],
                                           xinT[:, u, :], start=True, stop=True)
                ins.then_inc(s_bh_ps, 1)

            def output(i, u, first):
                n = UNROLL * i + u
                pe.wait_ge(s_bh, n + 1)
                if not (first and u < 2):
                    pe.wait_ge(s_y_rows, n - 1)
                for r in range(SLOTS // P):
                    for c in range(FC):
                        ins = nc.tensor.matmul(psum[:, 6 + u % 2, r * P:(r + 1) * P],
                                               hT[:, u, c, r * P:(r + 1) * P],
                                               wst[:, u, HID + c * D:HID + (c + 1) * D],
                                               start=(c == 0), stop=(c == FC - 1))
                ins.then_inc(s_bo_ps, 1)

            transpose_in(0, 0)

            def body(i, first, last):
                for u in range(UNROLL):
                    if u + 1 < UNROLL:
                        transpose_in(i, u + 1)
                    elif not last:
                        transpose_in(i + 1, 0)
                    hidden(i, u, first)
                    if u > 1:
                        output(i, u - 2, first)
                    elif not first:
                        output(i - 1, u + 2, False)

            over_steps(pe, body)
            output(NBLK // UNROLL - 1, UNROLL - 2, False)
            output(NBLK // UNROLL - 1, UNROLL - 1, False)

        def ffn0_scalar(act):
            phase1_done(act)
            act.wait_ge(s_w2, W2_LOADS)

            def route(i, first):
                for u in range(2):
                    g = 2 * i + u
                    act.wait_ge(s_xh1T_ps, g + 1)
                    if not (first and u == 0):
                        act.wait_ge(s_gate_ps, g)
                    nc.scalar.activation(xh1T[:, :], two01, ACT.Copy).then_inc(s_xh1T, 1)

            over_pairs(act, route)
            act.wait_ge(s_table, 3)

            def copy_in(i, u):
                n = UNROLL * i + u
                act.wait_ge(s_bT_ps, n + 1)
                if not (isinstance(i, int) and i == 0):
                    act.wait_ge(s_bh_ps, n - UNROLL + 1)
                nc.scalar.activation(xinT[:, u, :], psum[:, u % 2, 0:SLOTS], ACT.Copy).then_inc(s_bT, 1)

            copy_in(0, 0)

            def body(i, first, last):
                for u in range(UNROLL):
                    n = UNROLL * i + u
                    if u + 1 < UNROLL:
                        copy_in(i, u + 1)
                    elif not last:
                        copy_in(i + 1, 0)
                    e = act.value_load(expert_i[0:1, bass.ds(n, 1)], min_val=0, max_val=NE - 1)
                    act.wait_ge(s_bh_ps, n + 1)
                    if not first:
                        act.wait_ge(s_bo_ps, n - UNROLL + 1)
                    for c in range(FC):
                        ins = nc.scalar.activation(hT[:, u, c, :], psum[:, 2 + u, c * SLOTS:(c + 1) * SLOTS],
                                                   ACT.Gelu, bias=f0_b1[:, bass.ds(e * FC + c, 1)])
                    ins.then_inc(s_bh, 1)

            over_steps(act, body)

        ROUTE_LINKS = LN_LINKS + 1 + TOP2_LINKS + 4

        def ffn0_vector(dve):
            phase1_done(dve)
            dve.wait_ge(s_w2, W2_LOADS)
            dve.wait_ge(s_const2, CONST2)
            nc.vector.memset(emask[:, GT, :], 0.0).then_inc(s_chT, 1)
            nc.vector.tensor_copy(filled[:, :], region[:, :]).then_inc(s_chT, 1)
            nc.vector.tensor_scalar(pad_rows[:, :, D], pad_rows[:, :, D], float(PADS * P), None, ALU.add)\
                .then_inc(s_chT, 1)
            dve.wait_ge(s_chT, 3)
            ch = Chain(dve, s_chC, ROUTE_LINKS)

            def route(i, first):
                for u in range(2):
                    g = 2 * i + u
                    ch.body(g)
                    if not first:
                        dve.wait_ge(s_sent[u], 16 * TOPK * GT * i)
                    chained_layernorm(ch, lambda t: tile_of_x(g, t))
                    nc.vector.tensor_scalar(rows[:, u, :, D], token_no[:, bass.ds(g * GT, GT)], 1.0, None, ALU.mult)
                    for t in range(GT):
                        ins = nc.vector.tensor_scalar(rows[:, u, t, 0:D], tile_of_x(g, t), mean[:, t:t + 1],
                                                      rstd[:, t:t + 1], ALU.subtract, ALU.mult)
                    ins.then_inc(s_xh1, 1)
                    dve.wait_ge(s_gate_ps, g + 1)
                    ch.link(nc.vector.tensor_tensor(
                        gate[:, :, :], psum[:, 6, 0:GT * NE].rearrange("p (t e) -> p t e", e=NE),
                        f0_bg[:, :].unsqueeze(1).to_broadcast((P, GT, NE)), ALU.add))
                    top2(ch, gate[:, :, :], gate2[:, :, :], [hot[:, k, :, :] for k in range(TOPK)],
                         place[:, :, :], gmax[:, :], P, GT, rank8)
                    nc.vector.tensor_tensor(emask[:, 0:GT, :], hot[:, 0, :, :], hot[:, 1, :, :], ALU.add)\
                        .then_inc(s_mask, 1)
                    dve.wait_ge(s_mask, g + 1)
                    ch.link(nc.vector.tensor_tensor(place[:, :, :], emask[:, 0:GT, :],
                                                    rank8[:, :].unsqueeze(1).to_broadcast((P, GT, NE)), ALU.mult))
                    nc.vector.tensor_reduce(rows[:, u, :, D + 1], place[:, :, :], AX_X, ALU.max)
                    dve.wait_ge(s_rank_ps, g + 1)
                    ch.link(nc.vector.tensor_tensor(
                        pos[:, :, :], psum[:, 7, 0:GT * NE].rearrange("p (t e) -> p t e", e=NE),
                        filled[:, :].unsqueeze(1).to_broadcast((P, GT, NE)), ALU.add))
                    ch.mark(nc.vector.tensor_tensor(filled[:, :], filled[:, :], psum[:, 7, GT * NE:(GT + 1) * NE],
                                                    ALU.add))
                    ch.link(nc.vector.tensor_tensor(
                        posk[:, :, :, :], hot[:, :, :, :],
                        pos[:, :, :].unsqueeze(1).to_broadcast((P, TOPK, GT, NE)), ALU.mult))
                    with nc.allow_low_precision(reason="whole numbers below 2**24, all but one of each sum zero"):
                        nc.vector.tensor_reduce(row_of[:, u, :, :], posk[:, :, :, :], AX_X, ALU.add)\
                            .then_inc(s_rows, 1)
                    dve.wait_ge(s_rows, g + 1)

            over_pairs(dve, route)

            tb = Chain(dve, s_chT, 10000)
            tb.k = 3
            nc.vector.tensor_tensor(pad_at[:, :, :], pad_no[:, :, :],
                                    filled[:, :].unsqueeze(2).to_broadcast((P, NE, SLOTS // P)), ALU.add)\
                .then_inc(s_pads, 1)
            many = NT * P // SLOTS
            tb.link(nc.vector.tensor_tensor(total[:, :], filled[:, :], region[:, :], ALU.subtract))
            tb.link(nc.vector.tensor_tensor(full[:, :, :], total[:, :].unsqueeze(2).to_broadcast((P, NE, many)),
                                            block_lo[:, :].unsqueeze(1).to_broadcast((P, NE, many)), ALU.is_gt))
            tb.link(nc.vector.tensor_reduce(steps_of[:, :], full[:, :, :], AX_X, ALU.add))
            ends = steps_of
            for s, nxt in ((1, end_a), (2, end_b), (4, end_a)):
                tb.mark(nc.vector.tensor_copy(nxt[:, 0:s], ends[:, 0:s]))
                tb.link(nc.vector.tensor_tensor(nxt[:, s:NE], ends[:, s:NE], ends[:, 0:NE - s], ALU.add))
                ends = nxt
            tb.mark(nc.vector.tensor_scalar(skip[:, :], steps_of[:, :], -float(SLOTS), float(STRIDE),
                                            ALU.mult, ALU.add))
            tb.link(nc.vector.tensor_tensor(past[:, :, :], ends[:, :].unsqueeze(1).to_broadcast((P, NBLK, NE)),
                                            block_no[:, :].unsqueeze(2).to_broadcast((P, NBLK, NE)), ALU.is_le))
            tb.mark(nc.vector.tensor_tensor(passed[:, :, :], past[0:1, :, :],
                                            skip[0:1, :].unsqueeze(1).to_broadcast((1, NBLK, NE)), ALU.mult))
            tb.link(nc.vector.tensor_reduce(expert[:, :], past[:, :, :], AX_X, ALU.add))
            tb.link(nc.vector.tensor_reduce(row_f[:, :], passed[:, :, :], AX_X, ALU.add))
            nc.vector.scalar_tensor_tensor(row_i[:, :], block_no[0:1, :], float(SLOTS), row_f[:, :],
                                           ALU.mult, ALU.add).then_inc(s_table, 1)
            nc.vector.tensor_scalar(expert_i[:, :], expert[0:1, :], float(NE - 1), None, ALU.min).then_inc(s_table, 1)
            nc.vector.tensor_scalar(expert_rank[:, :], expert[:, :], -1.0, float(NE), ALU.mult, ALU.add)\
                .then_inc(s_table, 1)
            dve.wait_ge(s_table, 3)

            def stage_weights(i, u):
                n = UNROLL * i + u
                e = dve.value_load(expert_i[0:1, bass.ds(n, 1)], min_val=0, max_val=NE - 1)
                nc.vector.tensor_scalar(wst[:, u, :], f0_w[:, :, :].rearrange("p e n -> p (e n)")
                                        [:, bass.ds(e * (2 * HID), 2 * HID)], 1.0, None, ALU.mult).then_inc(s_wst, 1)

            def destinations(i, u, first):
                n = UNROLL * i + u
                dve.wait_ge(s_xin[u], 16 * i + 16)
                if not first:
                    dve.wait_ge(s_y_sent[u], 16 * (SLOTS // P) * i)
                nc.vector.tensor_scalar(higher[:, u, :], xin[:, u, :, D + 1], expert_rank[:, bass.ds(n, 1)],
                                        float(NT * P), ALU.is_gt, ALU.mult).then_inc(s_higher, 1)
                dve.wait_ge(s_higher, n + 1)
                nc.vector.tensor_tensor(y_at[:, u, :], xin[:, u, :, D], higher[:, u, :], ALU.add).then_inc(s_y_at, 1)

            def add_bias(i, u):
                n = UNROLL * i + u
                e = dve.value_load(expert_i[0:1, bass.ds(n, 1)], min_val=0, max_val=NE - 1)
                dve.wait_ge(s_bo_ps, n + 1)
                nc.vector.tensor_tensor(
                    y_rows[:, u, :, :], psum[:, 6 + u % 2, 0:SLOTS].rearrange("p (r d) -> p r d", d=D),
                    f0_b2[:, bass.ds(e * D, D)].unsqueeze(1).to_broadcast((P, SLOTS // P, D)), ALU.add)\
                    .then_inc(s_y_rows, 1)

            stage_weights(0, 0)
            stage_weights(0, 1)

            def body(i, first, last):
                for u in range(UNROLL):
                    destinations(i, u, first)
                    if u > 1:
                        add_bias(i, u - 2)
                    elif not first:
                        add_bias(i - 1, u + 2)
                    if u < 2:
                        stage_weights(i, u + 2)
                    elif not last:
                        stage_weights(i + 1, u - 2)

            over_steps(dve, body)
            add_bias(NBLK // UNROLL - 1, UNROLL - 2)
            add_bias(NBLK // UNROLL - 1, UNROLL - 1)

        def ffn0_gpsimd(pool):
            def route(i, first):
                for u in range(2):
                    pool.wait_ge(s_rows, 2 * i + u + 1)
                    pool.sem_inc(s_pool_step, 1)
                    for k in range(TOPK):
                        for t in range(GT):
                            pool.indirect_dma_start(
                                rows_dram[:, :], bass.IndirectOffsetOnAxis(ap=row_of[:, u, k, t:t + 1], axis=0),
                                rows[:, u, t, :], None).then_inc(s_sent[u], 16)

            over_pairs(pool, route)
            pool.wait_ge(s_pads, 1)
            for e in range(NE):
                for r in range(SLOTS // P):
                    pool.indirect_dma_start(
                        rows_dram[:, :], bass.IndirectOffsetOnAxis(ap=pad_at[:, e, r:r + 1], axis=0),
                        pad_rows[:, e * (SLOTS // P) + r, :], None).then_inc(s_padded, 16)

            def body(i, first, last):
                for u in range(UNROLL):
                    pool.wait_ge(s_y_rows, UNROLL * i + u + 1)
                    pool.sem_inc(s_pool_step, 1)
                    for r in range(SLOTS // P):
                        pool.indirect_dma_start(
                            y_dram[:, :], bass.IndirectOffsetOnAxis(ap=y_at[:, u, r:r + 1], axis=0),
                            y_rows[:, u, r, :], None).then_inc(s_y_sent[u], 16)

            over_steps(pool, body)

        ph2.close()

        xh3 = sb("xh3", [P, NT, D])
        xh3T = sb("xh3T", [P, NT * P])
        meanT = sb("meanT", [P, NB])
        f1_wr = sb("f1_wr", [P, NE])
        f1_br = sb("f1_br", [NB, NE])
        f1_w1 = sb("f1_w1", [P, NE * HID])
        f1_w2 = sb("f1_w2", [P, NE * FC * D])
        f1_b1 = sb("f1_b1", [P, NE, FC])
        f1_b2 = sb("f1_b2", [NE, D])
        gamma, beta = sb("gamma", [P, D]), sb("beta", [P, D])
        s_w4 = sem("s_w4")
        ph3 = ExitStack()
        ctx.push(ph3)

        def sb3(name, shape, dt=F32):
            return ph3.enter_context(nc.sbuf_tensor(name, shape, dt))

        ww = sb3("ww", [P, D])
        a_cols = sb3("a_cols", [P, 2])
        wb_col = sb3("wb_col", [P, 1])
        wb_row = sb3("wb_row", [P, D])
        wb_wide = sb3("wb_wide", [P, P])
        ab = sb3("ab", [P, 1])
        wh = sb3("wh", [P, D + 2])
        ef_bias = sb3("ef_bias", [P, 2])
        avg = sb3("avg", [P, 1])
        adjT2 = sb3("adjT2", [P, GB, 2, NN])
        xh2 = sb3("xh2", [P, GT, D])
        xh2T = sb3("xh2T", [P, GTOK])
        h_lin = sb3("h_lin", [P, GT, D])
        ef = sb3("ef", [P, GT, 2])
        expf = sb3("expf", [P, GT, 2])
        hf = sb3("hf", [P, GT, D + 1])
        den = sb3("den", [P, GT])
        h_new = sb3("h_new", [P, GT, D])
        xh3g = sb3("xh3g", [P, GT, D])

        y_in = sb3("y_in", [P, TOPK, GT, D])
        s_y_in = sem("s_y_in")
        s_w3, s_wwT_ps, s_init3 = sem("s_w3"), sem("s_wwT_ps"), sem("s_init3")
        s_adjT2 = sem("s_adjT2")
        s_xh2, s_xh2T_ps, s_xh2T, s_hl_ps = sem("s_xh2"), sem("s_xh2T_ps"), sem("s_xh2T"), sem("s_hl_ps")
        s_hlin, s_expf, s_hf, s_n_ps = sem("s_hlin"), sem("s_expf"), sem("s_hf"), sem("s_n_ps")
        s_hnew, s_x3, s_xh3g, s_xh3T_ps = sem("s_hnew"), sem("s_x3"), sem("s_xh3g"), sem("s_xh3T_ps")
        s_mean_ps, s_mean, s_xh3, s_xh3T = sem("s_mean_ps"), sem("s_mean"), sem("s_xh3"), sem("s_xh3T")
        s_chD, s_chE = sem("s_chD"), sem("s_chE")

        hl_ps = psum[:, 0:4, :].rearrange("p b (t n) -> p (b t) n", t=2)
        n_ps = psum[:, 4:8, :].rearrange("p b (t n) -> p (b t) n", t=2)
        two45 = psum[:, 4:6, :].rearrange("p a n -> p (a n)")

        def phase2_done(engine):
            for u in range(UNROLL):
                engine.wait_ge(s_y_sent[u], 16 * (SLOTS // P) * NBLK // UNROLL)

        def gnn1_sync(sp):
            phase2_done(sp)

            def load_y(g):
                for k in range(TOPK):
                    sp.dma_start(y_in[:, k, :, :], y_dram[bass.ds(k * NT * P + g * GTOK, GTOK), :]
                                 .rearrange("(t p) d -> p t d", p=P)).then_inc(s_y_in, 16)

            load_y(0)
            sp.dma_start(ww[:, :], I["L1_gnn_W_w"]).then_inc(s_w3, 16)
            with nc.allow_non_contiguous_dma(reason="256 values, two per partition"):
                sp.dma_start(a_cols[:, :], I["L1_gnn_a_w"].rearrange("(k e) -> e k", k=2)).then_inc(s_w3, 16)
            sp.dma_start(wb_col[:, :], I["L1_gnn_W_b"].rearrange("(p a) -> p a", a=1)).then_inc(s_w3, 16)
            sp.dma_start(wb_row[:, :], I["L1_gnn_W_b"].rearrange("(a n) -> a n", a=1).to_broadcast((P, D)))\
                .then_inc(s_w3, 16)
            sp.dma_start(ab[:, :], I["L1_gnn_a_b"].rearrange("(a n) -> a n", a=1).to_broadcast((P, 1)))\
                .then_inc(s_w3, 16)
            sp.dma_start(adjT2[:, :, :, :].rearrange("p b c n -> p (b c n)"), adjT_dram[0])\
                .then_inc(s_adjT2, 16)
            load_weights4(sp)
            with sp.Fori(1, NG) as g:
                sp.wait_ge(s_x2, TOPK * g)
                load_y(g)
                sp.wait_ge(s_adjT2, 16 * g)
                sp.wait_ge(s_n_ps, g)
                sp.dma_start(adjT2[:, :, :, :].rearrange("p b c n -> p (b c n)"), adjT_dram[g])\
                    .then_inc(s_adjT2, 16)

        W3_LOADS = 16 * 5

        def gnn1_tensor(pe):
            phase2_done(pe)
            pe.wait_ge(s_w3, W3_LOADS)
            pe.wait_ge(s_init3, 1)
            nc.tensor.transpose(psum[:, 0, 0:P], ww[:, :], ident[:, :]).then_inc(s_wwT_ps, 1)
            nc.tensor.matmul(psum[:, 1, 0:2], ww[:, :], a_cols[:, :], start=True, stop=True)\
                .then_inc(s_wwT_ps, 1)
            nc.tensor.matmul(psum[:, 2, 0:2], wb_wide[:, :], a_cols[:, :], start=True, stop=True)\
                .then_inc(s_wwT_ps, 1)
            pe.wait_ge(s_init3, 4)

            def body(g, a, b):
                if a:
                    pe.wait_ge(s_xh2, g + 1)
                    if b:
                        pe.wait_ge(s_hlin, 2 * g)
                    for t in range(GT):
                        ins = nc.tensor.transpose(two01[:, t * P:(t + 1) * P], xh2[:, t, :], ident[:, :])
                    ins.then_inc(s_xh2T_ps, 1)
                    pe.wait_ge(s_xh2T, g + 1)
                    for t in range(GT):
                        ins = nc.tensor.matmul(hl_ps[:, t, 0:D + 2], xh2T[:, t * P:(t + 1) * P], wh[:, :],
                                               start=True, stop=True)
                    ins.then_inc(s_hl_ps, 1)
                if b:
                    pe.wait_ge(s_xh3g, g)
                    for t in range(GT):
                        ins = nc.tensor.transpose(two45[:, t * P:(t + 1) * P], xh3g[:, t, :], ident[:, :])
                    ins.then_inc(s_xh3T_ps, 1)
                    for j in range(GB):
                        for r in range(2):
                            ins = nc.tensor.matmul(psum[:, 6, j:j + 1], xh3g[:, 2 * j + r, :], avg[:, :],
                                                   start=(r == 0), stop=(r == 1))
                    ins.then_inc(s_mean_ps, 1)
                if a:
                    pe.wait_ge(s_hf, 2 * g + 2)
                    pe.wait_ge(s_adjT2, 16 * (g + 1))
                    if b:
                        pe.wait_ge(s_mean, g + 1)
                        pe.wait_ge(s_xh3T, g)
                    for j in range(GB):
                        for r in range(2):
                            for c in range(2):
                                ins = nc.tensor.matmul(
                                    n_ps[:, 2 * j + r, 0:D + 1], adjT2[:, j, c, r * P:(r + 1) * P],
                                    hf[:, 2 * j + c, :], start=(c == 0), stop=(c == 1))
                    ins.then_inc(s_n_ps, 1)

            for_groups(pe, body)

        def gnn1_scalar(act):
            phase2_done(act)
            act.wait_ge(s_w3, W3_LOADS)
            nc.scalar.activation(act_token[:, :], ones[:, 0:1], ACT.Copy).then_inc(s_xh3, 1)

            def body(g, a, b):
                if a:
                    act.wait_ge(s_xh2T_ps, g + 1)
                    nc.scalar.activation(xh2T[:, :], two01, ACT.Copy).then_inc(s_xh2T, 1)
                if b:
                    act.wait_ge(s_xh3g, g)
                    nc.scalar.activation(xh3[:, bass.ds((g - 1) * GT, GT), :].rearrange("p t d -> p (t d)"),
                                         xh3g[:, :, :].rearrange("p t d -> p (t d)"), ACT.Copy)\
                        .then_inc(s_xh3, 1)
                    act.wait_ge(s_xh3T_ps, g)
                    nc.scalar.activation(xh3T[:, bass.ds((g - 1) * GTOK, GTOK)], two45, ACT.Copy)\
                        .then_inc(s_xh3T, 1)
                if a:
                    act.wait_ge(s_hlin, 2 * g + 2)
                    nc.scalar.activation(expf[:, :, :], ef[:, :, :], ACT.Exp).then_inc(s_expf, 1)

            for_groups(act, body)

        def gnn1_vector(dve):
            phase2_done(dve)
            dve.wait_ge(s_w3, W3_LOADS)
            nc.vector.memset(avg[:, :], 1.0 / NN).then_inc(s_mean, 1)
            nc.vector.tensor_scalar(wb_wide[:, :], ones[:, :], wb_col[:, 0:1], None, ALU.mult).then_inc(s_init3, 1)
            dve.wait_ge(s_wwT_ps, 3)
            nc.vector.tensor_copy(wh[:, 0:D], psum[:, 0, 0:P]).then_inc(s_init3, 1)
            nc.vector.tensor_copy(wh[:, D:D + 2], psum[:, 1, 0:2]).then_inc(s_init3, 1)
            nc.vector.tensor_copy(ef_bias[:, :], psum[:, 2, 0:2]).then_inc(s_init3, 1)
            dve.wait_ge(s_init3, 4)
            nc.vector.tensor_tensor(ef_bias[:, 0:1], ef_bias[:, 0:1], ab[:, :], ALU.add).then_inc(s_init3, 1)
            dve.wait_ge(s_init3, 5)
            chD = Chain(dve, s_chD, LN_LINKS)
            chE = Chain(dve, s_chE, LN_LINKS + 2)

            def body(g, a, b):
                if b:
                    chE.body(g - 1)
                    dve.wait_ge(s_n_ps, g)
                    chE.link(nc.vector.tensor_tensor(den[:, :], n_ps[:, :, D], expf[:, :, 0], ALU.mult))
                    chE.link(nc.vector.reciprocal(den[:, :], den[:, :]))
                    dve.wait_ge(s_x3, g)
                    for t in range(GT):
                        ins = nc.vector.tensor_scalar(h_new[:, t, :], n_ps[:, t, 0:D], expf[:, t, 0:1],
                                                      den[:, t:t + 1], ALU.mult, ALU.mult)
                    ins.then_inc(s_hnew, 1)
                if a:
                    chD.body(g)
                    dve.wait_ge(s_x2, TOPK * (g + 1))
                    chained_layernorm(chD, lambda t: tile_of_x(g, t))
                    if b:
                        dve.wait_ge(s_xh2T_ps, g)
                    for t in range(GT):
                        ins = nc.vector.tensor_scalar(xh2[:, t, :], tile_of_x(g, t), mean[:, t:t + 1],
                                                      rstd[:, t:t + 1], ALU.subtract, ALU.mult)
                    ins.then_inc(s_xh2, 1)
                    dve.wait_ge(s_xh2, g + 1)
                if b:
                    dve.wait_ge(s_x3, g + 1)
                    chained_layernorm(chE, lambda t: tile_of_x(g - 1, t))
                    dve.wait_ge(s_xh3, g)
                    dve.wait_ge(s_mean, g)
                    for t in range(GT):
                        ins = nc.vector.tensor_scalar(xh3g[:, t, :], tile_of_x(g - 1, t), mean[:, t:t + 1],
                                                      rstd[:, t:t + 1], ALU.subtract, ALU.mult)
                    ins.then_inc(s_xh3g, 1)
                    dve.wait_ge(s_xh3g, g)
                if a:
                    dve.wait_ge(s_hl_ps, g + 1)
                    nc.vector.tensor_tensor(h_lin[:, :, :], hl_ps[:, :, 0:D],
                                            wb_row[:, :].unsqueeze(1).to_broadcast((P, GT, D)), ALU.add)\
                        .then_inc(s_hlin, 1)
                    nc.vector.tensor_tensor(ef[:, :, :], hl_ps[:, :, D:D + 2],
                                            ef_bias[:, :].unsqueeze(1).to_broadcast((P, GT, 2)), ALU.add)\
                        .then_inc(s_hlin, 1)
                    dve.wait_ge(s_expf, g + 1)
                    nc.vector.tensor_tensor(hf[:, :, 0:D], h_lin[:, :, :],
                                            expf[:, :, 1:2].to_broadcast((P, GT, D)), ALU.mult).then_inc(s_hf, 1)
                    nc.vector.tensor_copy(hf[:, :, D], expf[:, :, 1]).then_inc(s_hf, 1)
                if b:
                    dve.wait_ge(s_mean_ps, g)
                    nc.vector.tensor_copy(meanT[:, bass.ds((g - 1) * GB, GB)], psum[:, 6, 0:GB]).then_inc(s_mean, 1)

            for_groups(dve, body)

        def gnn1_gpsimd(pool):
            phase2_done(pool)
            pool.wait_ge(s_w3, W3_LOADS)
            nc.gpsimd.memset(pool_token[:, :], 0.0).then_inc(s_x3, 1)

            def add_experts(g):
                pool.wait_ge(s_y_in, 16 * TOPK * (g + 1))
                nc.gpsimd.tensor_tensor(y_in[:, 0, :, :], y_in[:, 0, :, :], y_in[:, 1, :, :], ALU.add)\
                    .then_inc(s_x2, 1)
                pool.wait_ge(s_x2, TOPK * g + 1)
                xg = xres[:, bass.ds(g * GT, GT), :]
                nc.gpsimd.tensor_tensor(xg, y_in[:, 0, :, :], xg, ALU.add).then_inc(s_x2, 1)

            def add_attention(g):
                pool.wait_ge(s_hnew, g + 1)
                xg = xres[:, bass.ds(g * GT, GT), :]
                nc.gpsimd.tensor_tensor(xg, h_new[:, :, :], xg, ALU.add).then_inc(s_x3, 1)

            add_experts(0)
            with pool.Fori(1, NG) as g:
                add_experts(g)
                pool.wait_ge(s_x2, TOPK * g + TOPK)
                add_attention(g - 1)
            add_attention(NG - 1)

        ph3.close()

        def load_weights4(sp):
            sp.dma_start(f1_wr[:, :], I["L1_ffn_Wr"]).then_inc(s_w4, 16)
            sp.dma_start(f1_w1[:, :].rearrange("p (e h) -> p e h", e=NE), I["L1_ffn_W1"].rearrange("e d h -> d e h"))\
                .then_inc(s_w4, 16)
            sp.dma_start(f1_w2[:, :].rearrange("p (e c d) -> p e c d", e=NE, c=FC),
                         I["L1_ffn_W2"].rearrange("e (c p) d -> p e c d", p=P)).then_inc(s_w4, 16)
            with nc.allow_non_contiguous_dma(reason="2048 biases, one per partition"):
                for e in range(NE):
                    sp.dma_start(f1_b1[:, e, :], I["L1_ffn_b1"][e].rearrange("(c p) -> p c", p=P))\
                        .then_inc(s_w4, 16)
            sp.dma_start(f1_b2[:, :], I["L1_ffn_b2"]).then_inc(s_w4, 16)
            for dst, name, rows in ((f1_br, "L1_ffn_br", NB), (gamma, "L1_ffn_gamma", P), (beta, "L1_ffn_beta", P)):
                sp.dma_start(dst[:, :], I[name].rearrange("(a n) -> a n", a=1)
                             .to_broadcast((rows, dst.shape[1]))).then_inc(s_w4, 16)

        W4_LOADS = 16 * (3 + NE + 4)

        ph4 = ExitStack()
        ctx.push(ph4)

        def sb4(name, shape, dt=F32):
            return ph4.enter_context(nc.sbuf_tensor(name, shape, dt))

        logit = sb4("logit", [NB, NE])
        rexp = sb4("rexp", [NB, NE])
        rw = sb4("rw", [NB, NE])
        rw2 = sb4("rw2", [NB, 1, NE])
        rw2b = sb4("rw2b", [NB, 1, NE])
        rplace = sb4("rplace", [NB, 1, NE])
        scale = sb4("scale", [NB, NE])
        rmax = sb4("rmax", [NB, 1])
        rsum = sb4("rsum", [NB, 1])
        hot4 = sb4("hot4", [NB, TOPK, NE])
        first_row = sb4("first_row", [NB, NE])
        picked = sb4("picked", [NB, TOPK, NE])
        topw = sb4("topw", [NB, TOPK])
        topd = sb4("topd", [NB, 1])
        info = sb4("info", [NB, 2 * TOPK])
        wdense = sb4("wdense", [NB, NE])
        wd2 = sb4("wd2", [NB, NE])
        info_diag = sb4("info_diag", [NB, 2 * TOPK, NB])
        hot_diag = sb4("hot_diag", [NB, TOPK * NE, NB])
        wtok = sb4("wtok", [P, TOPK, NB])
        places = sb4("places", [1, TOPK, NB], I32)
        b1prod = sb4("b1prod", [P, TOPK * FC, NB, NE])
        b1sel = sb4("b1sel", [P, TOPK * FC, NB])
        wdT = sb4("wdT", [NE, NB])
        SLOTS4 = GB
        w1s = sb4("w1s", [P, SLOTS4, TOPK, HID])
        w2s = sb4("w2s", [P, SLOTS4, TOPK, FC * D])
        hT4 = sb4("hT4", [P, 2, TOPK, FC, NN])
        wb2 = sb4("wb2", [NE, GB, D])
        b2r = sb4("b2r", [P, GB, D])
        z = sb4("z", [P, GT, D])
        yout = sb4("yout", [P, GT, D])

        s_r_ps, s_r = sem("s_r_ps"), sem("s_r")
        s_rin, s_rexp = sem("s_rin"), sem("s_rexp")
        s_chR, s_chF = sem("s_chR"), sem("s_chF")
        s_info, s_wd, s_sel_ps, s_wtok, s_places, s_b1sel, s_wdT = (
            sem("s_info"), sem("s_wd"), sem("s_sel_ps"), sem("s_wtok"), sem("s_places"), sem("s_b1sel"), sem("s_wdT"))
        s_w1s, s_w2s, s_h4_ps, s_h4, s_o_ps, s_z = (
            sem("s_w1s"), sem("s_w2s"), sem("s_h4_ps"), sem("s_h4"), sem("s_o_ps"), sem("s_z"))
        s_wb2, s_b2r_ps, s_b2r, s_xb = sem("s_wb2"), sem("s_b2r_ps"), sem("s_b2r"), sem("s_xb")
        s_zs, s_yout = sem("s_zs"), sem("s_yout")

        CAPACITY = float(-(-NB * NN * 5 // (4 * NE)))

        def phase3_done(engine):
            engine.wait_ge(s_mean, NG + 1)
            engine.wait_ge(s_x3, NG + 1)
            engine.wait_ge(s_xh3, NG + 1)
            engine.wait_ge(s_xh3T, NG)
            engine.wait_ge(s_w4, W4_LOADS)

        def over_groups(engine, body):
            body(0, True, False)
            with engine.Fori(1, NG - 1) as g:
                body(g, False, False)
            body(NG - 1, False, True)

        def ffn1_sync(sp):
            with sp.Fori(0, NG) as g:
                sp.wait_ge(s_yout, g + 1)
                sp.dma_start(out_dram[g], yout[:, :, :]).then_inc(s_out, 16)
            sp.wait_ge(s_out, 16 * NG)

        def ffn1_tensor(pe):
            phase3_done(pe)
            nc.tensor.matmul(psum[0:NB, 0, 0:NE], meanT[:, :], f1_wr[:, :], start=True, stop=True)\
                .then_inc(s_r_ps, 1)
            pe.wait_ge(s_r, 1)
            nc.tensor.matmul(psum[0:NB, 1, 0:NE], ones[0:NB, 0:NB], rw[:, :], start=True, stop=True)\
                .then_inc(s_r_ps, 1)
            pe.wait_ge(s_info, 2)
            nc.tensor.matmul(psum[:, 2, 0:2 * TOPK * NB], ones[0:NB, :],
                             info_diag[:, :, :].rearrange("p k b -> p (k b)"), start=True, stop=True)\
                .then_inc(s_sel_ps, 1)
            nc.tensor.matmul(psum[:, 3, 0:TOPK * NE * NB], ones[0:NB, :],
                             hot_diag[:, :, :].rearrange("p k b -> p (k b)"), start=True, stop=True)\
                .then_inc(s_sel_ps, 1)
            pe.wait_ge(s_wd, 1)
            nc.tensor.transpose(psum[0:NE, 4, 0:NB], wdense[:, :], ident[0:NB, 0:NB]).then_inc(s_sel_ps, 1)

            def spread_b2(g):
                pe.wait_ge(s_wb2, g + 1)
                nc.tensor.matmul(psum[:, 6, 0:GB * D], ones[0:NE, :], wb2[:, :, :].rearrange("p b d -> p (b d)"),
                                 start=True, stop=True).then_inc(s_b2r_ps, 1)

            def hidden(g, j, first):
                n = GB * g + j
                pe.wait_ge(s_w1s, n + 1)
                if not (first and j < 2):
                    pe.wait_ge(s_h4, TOPK * FC * (n - 1))
                for k in range(TOPK):
                    for c in range(FC):
                        ins = nc.tensor.matmul(psum[:, 2 * (j % 2) + k, c * NN:(c + 1) * NN],
                                               w1s[:, j, k, c * P:(c + 1) * P],
                                               xh3T[:, bass.ds(g * GTOK + j * NN, NN)], start=True, stop=True)
                    ins.then_inc(s_h4_ps, 1)

            def output(g, j, first):
                n = GB * g + j
                pe.wait_ge(s_h4, TOPK * FC * (n + 1))
                pe.wait_ge(s_w2s, n + 1)
                if not (first and j < 2):
                    pe.wait_ge(s_z, n - 1)
                for r in range(2):
                    for i in range(TOPK * FC):
                        k, c = divmod(i, FC)
                        ins = nc.tensor.matmul(psum[:, 4 + j % 2, r * P:(r + 1) * P],
                                               hT4[:, j % 2, k, c, r * P:(r + 1) * P],
                                               w2s[:, j, k, c * D:(c + 1) * D],
                                               start=(i == 0), stop=(i == TOPK * FC - 1))
                ins.then_inc(s_o_ps, 1)

            pe.wait_ge(s_wdT, 1)
            pe.wait_ge(s_b1sel, 1)
            pe.wait_ge(s_wtok, 1)
            pe.wait_ge(s_places, 1)

            def body(g, first, last):
                spread_b2(g)
                for j in range(GB):
                    hidden(g, j, first)
                    if j > 0:
                        output(g, j - 1, first)
                    elif not first:
                        output(g - 1, GB - 1, False)
                if last:
                    output(g, GB - 1, False)

            over_groups(pe, body)

        def ffn1_scalar(act):
            phase3_done(act)
            for i, (src, dst) in enumerate(((logit[:, :], rexp[:, :]), (logit[:, :], rexp[:, :]),
                                            (topd[:, :], topd[:, :]))):
                act.wait_ge(s_rin, i + 1)
                nc.scalar.activation(dst, src, ACT.Exp).then_inc(s_rexp, 1)
            act.wait_ge(s_b1sel, 1)

            def body(g, first, last):
                act.wait_ge(s_b2r_ps, g + 1)
                if not first:
                    act.wait_ge(s_xb, g)
                nc.scalar.activation(b2r[:, :, :].rearrange("p b d -> p (b d)"), psum[:, 6, 0:GB * D], ACT.Copy)\
                    .then_inc(s_b2r, 1)
                for j in range(GB):
                    n = GB * g + j
                    for k in range(TOPK):
                        act.wait_ge(s_h4_ps, TOPK * n + k + 1)
                        if k == 0 and not (first and j < 2):
                            act.wait_ge(s_o_ps, n - 1)
                        for c in range(FC):
                            nc.scalar.activation(hT4[:, j % 2, k, c, :], psum[:, 2 * (j % 2) + k, c * NN:(c + 1) * NN],
                                                 ACT.Gelu, bias=b1sel[:, FC * k + c, bass.ds(g * GB + j, 1)])\
                                .then_inc(s_h4, 1)

            over_groups(act, body)

        LN4_LINKS = LN_LINKS + GT

        def ffn1_vector(dve):
            phase3_done(dve)
            ch = Chain(dve, s_chR, 10000)
            for e in range(NE):
                ch.mark(nc.vector.memset(first_row[:, e:e + 1], float(e * HID)))

            def softmax(values, dst):
                softmax.calls += 1
                ch.link(nc.vector.tensor_reduce(rmax[:, :], values, AX_X, ALU.max))
                nc.vector.tensor_scalar(logit[:, :], values, rmax[:, 0:1], None, ALU.subtract).then_inc(s_rin, 1)
                dve.wait_ge(s_rexp, softmax.calls)
                ch.link(nc.vector.tensor_reduce(rsum[:, :], rexp[:, :], AX_X, ALU.add))
                ch.link(nc.vector.reciprocal(rsum[:, :], rsum[:, :]))
                return nc.vector.tensor_scalar(dst, rexp[:, :], rsum[:, 0:1], None, ALU.mult)

            softmax.calls = 0
            dve.wait_ge(s_r_ps, 1)
            ch.link(nc.vector.tensor_tensor(rexp[:, :], psum[0:NB, 0, 0:NE], f1_br[:, :], ALU.add))
            softmax(rexp[:, :], rw[:, :]).then_inc(s_r, 1)
            dve.wait_ge(s_r, 1)
            dve.wait_ge(s_r_ps, 2)
            ch.link(nc.vector.reciprocal(scale[:, :], psum[0:NB, 1, 0:NE]))
            ch.link(nc.vector.tensor_scalar(scale[:, :], scale[:, :], CAPACITY / NN, 1.0, ALU.mult, ALU.min))
            ch.link(nc.vector.tensor_tensor(rw[:, :], rw[:, :], scale[:, :], ALU.mult))
            ch.link(softmax(rw[:, :], rw2[:, 0, :]))
            top2(ch, rw2[:, :, :], rw2b[:, :, :], [hot4[:, k:k + 1, :] for k in range(TOPK)],
                 rplace[:, :, :], rmax[:, :], NB, 1, rank8)
            ch.link(nc.vector.tensor_tensor(picked[:, :, :], hot4[:, :, :],
                                            rw2[:, 0:1, :].to_broadcast((NB, TOPK, NE)), ALU.mult))
            ch.link(nc.vector.tensor_reduce(topw[:, :], picked[:, :, :], AX_X, ALU.add))
            nc.vector.tensor_tensor(topd[:, :], topw[:, 1:2], topw[:, 0:1], ALU.subtract).then_inc(s_rin, 1)
            ch.link(nc.vector.tensor_tensor(picked[:, :, :], hot4[:, :, :],
                                            first_row[:, :].unsqueeze(1).to_broadcast((NB, TOPK, NE)), ALU.mult))
            ch.link(nc.vector.tensor_reduce(info[:, TOPK:2 * TOPK], picked[:, :, :], AX_X, ALU.add))
            nc.vector.tensor_tensor(hot_diag[:, :, :],
                                    hot4[:, :, :].rearrange("p k e -> p (k e)").unsqueeze(2)
                                    .to_broadcast((NB, TOPK * NE, NB)),
                                    ident[0:NB, 0:NB].unsqueeze(1).to_broadcast((NB, TOPK * NE, NB)), ALU.mult)\
                .then_inc(s_info, 1)
            dve.wait_ge(s_rexp, 3)
            ch.link(nc.vector.tensor_scalar(rsum[:, :], topd[:, :], 1.0, None, ALU.add))
            ch.link(nc.vector.reciprocal(info[:, 0:1], rsum[:, :]))
            ch.link(nc.vector.tensor_tensor(info[:, 1:2], topd[:, :], info[:, 0:1], ALU.mult))
            nc.vector.tensor_tensor(info_diag[:, :, :], info[:, :].unsqueeze(2).to_broadcast((NB, 2 * TOPK, NB)),
                                    ident[0:NB, 0:NB].unsqueeze(1).to_broadcast((NB, 2 * TOPK, NB)), ALU.mult)\
                .then_inc(s_info, 1)
            ch.link(nc.vector.tensor_scalar(wd2[:, :], hot4[:, 0, :], info[:, 0:1], None, ALU.mult))
            nc.vector.scalar_tensor_tensor(wdense[:, :], hot4[:, 1, :], info[:, 1:2], wd2[:, :],
                                           ALU.mult, ALU.add).then_inc(s_wd, 1)
            dve.wait_ge(s_sel_ps, 1)
            nc.vector.tensor_copy(places[:, :, :], psum[0:1, 2, TOPK * NB:2 * TOPK * NB]
                                  .rearrange("p (k b) -> p k b", k=TOPK)).then_inc(s_places, 1)
            nc.vector.tensor_copy(wtok[:, :, :], psum[:, 2, 0:TOPK * NB].rearrange("p (k b) -> p k b", k=TOPK))\
                .then_inc(s_wtok, 1)
            dve.wait_ge(s_sel_ps, 2)
            for k in range(TOPK):
                for c in range(FC):
                    ch.mark(nc.vector.tensor_tensor(
                        b1prod[:, FC * k + c, :, :],
                        psum[:, 3, k * NE * NB:(k + 1) * NE * NB].rearrange("p (e b) -> p b e", e=NE),
                        f1_b1[:, :, c].unsqueeze(1).to_broadcast((P, NB, NE)), ALU.mult))
            ch.settle()
            nc.vector.tensor_reduce(b1sel[:, :, :], b1prod[:, :, :, :], AX_X, ALU.add).then_inc(s_b1sel, 1)
            dve.wait_ge(s_sel_ps, 3)
            nc.vector.tensor_copy(wdT[:, :], psum[0:NE, 4, 0:NB]).then_inc(s_wdT, 1)
            dve.wait_ge(s_places, 1)
            dve.wait_ge(s_wtok, 1)

            def stage_w2(g, j):
                for k in range(TOPK):
                    place = dve.value_load(places[0:1, k, bass.ds(g * GB + j, 1)], min_val=0, max_val=(NE - 1) * HID)
                    ins = nc.vector.tensor_scalar(w2s[:, j, k, :], f1_w2[:, bass.ds(place, FC * D)],
                                                  wtok[:, k, bass.ds(g * GB + j, 1)], None, ALU.mult)
                ins.then_inc(s_w2s, 1)

            for j in range(GB):
                stage_w2(0, j)

            chF = Chain(dve, s_chF, LN4_LINKS)

            def body(g, first, last):
                chF.body(g)
                dve.wait_ge(s_xb, g + 1)
                if not first:
                    dve.wait_ge(s_yout, g)
                for j in range(GB):
                    n = GB * g + j
                    dve.wait_ge(s_o_ps, n + 1)
                    nc.vector.tensor_tensor(z[:, 2 * j:2 * j + 2, :].rearrange("p t d -> p (t d)"),
                                            psum[:, 4 + j % 2, 0:NN],
                                            xh3[:, bass.ds(g * GT + 2 * j, 2), :].rearrange("p t d -> p (t d)"),
                                            ALU.add).then_inc(s_z, 1)
                    if not last:
                        stage_w2(g + 1, j)
                dve.wait_ge(s_z, GB * g + GB)
                chained_layernorm(chF, lambda t: z[:, t, :])
                for t in range(GT):
                    chF.mark(nc.vector.scalar_tensor_tensor(z[:, t, :], z[:, t, :], mean[:, t:t + 1], gamma[:, :],
                                                            ALU.subtract, ALU.mult))
                if not first:
                    dve.wait_ge(s_out, 16 * g)
                chF.settle()
                for t in range(GT):
                    ins = nc.vector.scalar_tensor_tensor(yout[:, t, :], z[:, t, :], rstd[:, t:t + 1],
                                                         tile_of_x(g, t), ALU.mult, ALU.add)
                ins.then_inc(s_yout, 1)

            over_groups(dve, body)

        def ffn1_gpsimd(pool):
            phase3_done(pool)
            pool.wait_ge(s_places, 1)

            def stage_w1(g, j):
                for k in range(TOPK):
                    place = pool.value_load(places[0:1, k, bass.ds(g * GB + j, 1)], min_val=0, max_val=(NE - 1) * HID)
                    ins = nc.gpsimd.tensor_copy(w1s[:, j, k, :], f1_w1[:, bass.ds(place, HID)])
                ins.then_inc(s_w1s, 1)

            def weigh_b2(g, first):
                if first:
                    pool.wait_ge(s_wdT, 1)
                else:
                    pool.wait_ge(s_b2r_ps, g)
                nc.gpsimd.tensor_tensor(wb2[:, :, :],
                                        wdT[:, bass.ds(g * GB, GB)].unsqueeze(2).to_broadcast((NE, GB, D)),
                                        f1_b2[:, :].unsqueeze(1).to_broadcast((NE, GB, D)), ALU.mult)\
                    .then_inc(s_wb2, 1)

            def add_biases(g):
                pool.wait_ge(s_b2r, g + 1)
                xg = xres[:, bass.ds(g * GT, GT), :]
                nc.gpsimd.tensor_tensor(xg, xg, beta[:, :].unsqueeze(1).to_broadcast((P, GT, D)), ALU.add)
                for r in range(2):
                    xb = xh3[:, bass.ds(g * GT, GT), :].rearrange("p (b r) d -> p b r d", r=2)[:, :, r, :]
                    ins = nc.gpsimd.tensor_tensor(xb, xb, b2r[:, :, :], ALU.add)
                ins.then_inc(s_xb, 1)

            for j in range(GB):
                stage_w1(0, j)
            weigh_b2(0, True)

            def body(g, first, last):
                add_biases(g)
                if not last:
                    weigh_b2(g + 1, False)
                    for j in range(GB):
                        pool.wait_ge(s_h4_ps, TOPK * (GB * g + j + 1))
                        stage_w1(g + 1, j)

            over_groups(pool, body)

        block = ctx.enter_context(nc.Block())

        @block.sync
        def _(sp):
            gnn0_sync(sp)
            sp.wait_ge(s_adjT_out, 16 * NG)
            ffn0_sync(sp)
            gnn1_sync(sp)
            ffn1_sync(sp)

        @block.gpsimd
        def _(pool):
            nc.gpsimd.memset(ident[:, :], 0.0).then_inc(s_poolc, 1)
            nc.gpsimd.memset(ones[:, :], 1.0).then_inc(s_const, 1)
            pool.wait_ge(s_poolc, 1)
            nc.gpsimd.affine_select(out=ident[:, :], in_=ident[:, :], compare_op=ALU.not_equal, fill=1.0,
                                    base=0, pattern=[[-1, P]], channel_multiplier=1).then_inc(s_const, 1)
            tables = (
                (token_no[:, :], [[P, NT]], 0, 1),
                (region[:, :], [[STRIDE, NE]], 0, 0),
                (block_no[:, :], [[1, NBLK]], 0, 0),
                (block_lo[:, :], [[SLOTS, NT * P // SLOTS]], 0, 0),
                (pad_no[:, :, :], [[0, NE], [P, SLOTS // P]], 0, 1),
                (pad_rows[:, :, D], [[P, PADS]], JUNK, 1),
            )
            for dst, pattern, base, step in tables:
                nc.gpsimd.iota(dst, pattern, base=base, channel_multiplier=step,
                               allow_small_or_imprecise_dtypes=True).then_inc(s_const2, 1)
            pool.wait_ge(s_const, 3)
            nc.gpsimd.affine_select(out=before[:, :], in_=ones[:, :], compare_op=ALU.is_gt, fill=0.0,
                                    base=0, pattern=[[1, P]], channel_multiplier=-1).then_inc(s_const2, 1)
            gnn0_gpsimd(pool)
            ffn0_gpsimd(pool)
            gnn1_gpsimd(pool)
            ffn1_gpsimd(pool)

        @block.tensor
        def _(pe):
            gnn0_tensor(pe)
            ffn0_tensor(pe)
            gnn1_tensor(pe)
            ffn1_tensor(pe)

        @block.scalar
        def _(act):
            gnn0_scalar(act)
            ffn0_scalar(act)
            gnn1_scalar(act)
            ffn1_scalar(act)

        @block.vector
        def _(dve):
            nc.vector.memset(kheadT[:, :, :], 0.0).then_inc(s_const, 1)
            nc.vector.memset(pad_rows[:, :, 0:D], 0.0)
            nc.vector.memset(pad_rows[:, :, D + 1], 0.0).then_inc(s_const2, 1)
            for e in range(NE):
                nc.vector.memset(rank8[:, e:e + 1], float(NE - e))
            gnn0_vector(dve)
            ffn0_vector(dve)
            gnn1_vector(dve)
            ffn1_vector(dve)


_INS = ["x", "adj", "L0_gnn_W_lin", "L0_gnn_b_lin", "L0_gnn_W_q", "L0_gnn_W_k", "L0_gnn_ln_g", "L0_gnn_ln_b",
        "L0_ffn_Wg", "L0_ffn_bg", "L0_ffn_W1", "L0_ffn_b1", "L0_ffn_W2", "L0_ffn_b2",
        "L1_gnn_W_w", "L1_gnn_W_b", "L1_gnn_a_w", "L1_gnn_a_b",
        "L1_ffn_Wr", "L1_ffn_br", "L1_ffn_W1", "L1_ffn_b1", "L1_ffn_W2", "L1_ffn_b2",
        "L1_ffn_gamma", "L1_ffn_beta"]
_OUTS = [((NB, NN, D), "float32")]


def kernel(**inputs):
    import numpy as _np
    import concourse.bacc as _bacc
    from concourse import mybir as _mybir
    from concourse.bass_utils import run_bass_kernel_spmd as _run

    nc = _bacc.Bacc("TRN2", target_bir_lowering=False, num_devices=1)
    arrays, tensors = {}, {}
    for name in _INS:
        a = _np.ascontiguousarray(inputs[name])
        arrays[f"in_{name}_dram"] = a
        tensors[name] = nc.dram_tensor(f"in_{name}_dram", a.shape, _mybir.dt.from_np(a.dtype),
                                       kind="ExternalInput").ap()
    outs = [nc.dram_tensor(f"out_{i}_dram", shape, _mybir.dt.from_np(_np.dtype(dtype)), kind="ExternalOutput").ap()
            for i, (shape, dtype) in enumerate(_OUTS)]
    build_program(nc, tensors, outs[0])
    r = _run(nc, [arrays], core_ids=[0])
    got = tuple(r.results[0][f"out_{i}_dram"] for i in range(len(_OUTS)))
    return got[0]
```
